# Optimizing a Trainium2 kernel written in Bass

```python
import numpy as np
import jax
import jax.numpy as jnp

def _softmax(x, axis=-1):
    return jax.nn.softmax(x, axis=axis)

def _gelu(x):
    return jax.nn.gelu(x, approximate=True)

def _silu(x):
    return jax.nn.silu(x)

def _sigmoid(x):
    return jax.nn.sigmoid(x)

def _layernorm(x, axis=-1, eps=1e-05):
    m = jnp.mean(x, axis=axis, keepdims=True)
    v = jnp.var(x, axis=axis, keepdims=True)
    return (x - m) / jnp.sqrt(v + eps)

def _scatter_add(tgt, idx, src, axis=0):
    return tgt.at[idx].add(src)

def _segment_sum(src, seg, n):
    return jax.ops.segment_sum(src, seg, n)
kernel_name = 'mk_gnn_resnorm_d2_gnn_r8_173e5e'

def setup_inputs(seed: int=0):
    np.random.seed(seed)
    _w = jnp.asarray

    def _rec_inputs():
        import jax
        import jax.numpy as jnp
        _gk = jax.random.key(seed)
        x = -0.000202 + 1 * jax.random.normal(jax.random.fold_in(_gk, 1), (6250, 128), jnp.float32)
        src = jax.random.randint(jax.random.fold_in(_gk, 2), (200000,), 0, 6250, jnp.int32)
        dst = jnp.minimum((6250 * jax.random.uniform(jax.random.fold_in(_gk, 3), (200000,)) ** 2.0).astype(jnp.int32), 49999)
        _o = jnp.argsort(dst, stable=True)
        src = src[_o]
        dst = dst[_o]
        return (x, src, dst)
    x, src, dst = _rec_inputs()

    def _L0_gnn_setup():
        import jax, jax.numpy as jnp
        import numpy as np
        N_NODES = 6250
        N_EDGES = 100000
        D_IN = 128
        U = 128
        H = 128
        key = jax.random.key(seed)
        ks = jax.random.split(key, 8)
        s = lambda d: 1.0 / np.sqrt(d)
        x = jax.random.normal(ks[0], (N_NODES, D_IN), dtype=jnp.float32)
        edge_index = jax.random.randint(ks[1], (2, N_EDGES), 0, N_NODES, dtype=jnp.int64)
        W1 = jax.random.normal(ks[2], (D_IN, U), dtype=jnp.float32) * s(D_IN)
        b1 = jax.random.normal(ks[3], (U,), dtype=jnp.float32) * 0.01
        W2 = jax.random.normal(ks[4], (2 * U, H), dtype=jnp.float32) * s(2 * U)
        b2 = jax.random.normal(ks[5], (H,), dtype=jnp.float32) * 0.01
        W3 = jax.random.normal(ks[6], (H, H), dtype=jnp.float32) * s(H)
        b3 = jax.random.normal(ks[7], (H,), dtype=jnp.float32) * 0.01
        return {'x': x, 'edge_index': edge_index, 'W1': W1, 'b1': b1, 'W2': W2, 'b2': b2, 'W3': W3, 'b3': b3}
    _L0_gnn_all = _L0_gnn_setup()
    _L0_gnn_in = {k: v for k, v in _L0_gnn_all.items() if k in ('W1', 'b1', 'W2', 'b2', 'W3', 'b3')}
    del _L0_gnn_all

    def _L1_gnn_setup():
        import jax, jax.numpy as jnp
        import numpy as np
        NEG_SLOPE = 0.2

        def _gat_conv(x, W, att_src, att_dst, bias, src, dst, n_nodes):
            h = x @ W
            a_src = h @ att_src
            a_dst = h @ att_dst
            e = a_src[src] + a_dst[dst]
            e = jnp.where(e > 0, e, NEG_SLOPE * e)
            m = jax.ops.segment_max(e, dst, num_segments=n_nodes)
            ex = jnp.exp(e - m[dst])
            denom = jax.ops.segment_sum(ex, dst, num_segments=n_nodes)
            alpha = ex / denom[dst]
            msg = alpha[:, None] * h[src]
            out = jax.ops.segment_sum(msg, dst, num_segments=n_nodes)
            return out + bias
        key = jax.random.key(seed)
        ks = jax.random.split(key, 12)
        N, E, F_in, H, F_out = (6250, 100000, 128, 128, 128)

        def glorot(k, shape):
            lim = float(np.sqrt(6.0 / sum(shape))) if len(shape) > 1 else float(np.sqrt(6.0 / shape[0]))
            return jax.random.uniform(k, shape, jnp.float32, -lim, lim)
        return {'x': jax.random.normal(ks[0], (N, F_in), jnp.float32), 'edge_index': jax.random.randint(ks[1], (2, E), 0, N, jnp.int64), 'W1': glorot(ks[2], (F_in, H)), 'att_src1': glorot(ks[3], (H,)), 'att_dst1': glorot(ks[4], (H,)), 'b1': jnp.zeros((H,), jnp.float32), 'W2': glorot(ks[5], (H, F_out)), 'att_src2': glorot(ks[6], (F_out,)), 'att_dst2': glorot(ks[7], (F_out,)), 'b2': jnp.zeros((F_out,), jnp.float32)}
    _L1_gnn_all = _L1_gnn_setup()
    _L1_gnn_in = {k: v for k, v in _L1_gnn_all.items() if k in ('W1', 'att_src1', 'att_dst1', 'b1', 'W2', 'att_src2', 'att_dst2', 'b2')}
    del _L1_gnn_all
    return {'x': x, 'src': src, 'dst': dst, 'L0_gnn_W1': _L0_gnn_in['W1'], 'L0_gnn_b1': _L0_gnn_in['b1'], 'L0_gnn_W2': _L0_gnn_in['W2'], 'L0_gnn_b2': _L0_gnn_in['b2'], 'L0_gnn_W3': _L0_gnn_in['W3'], 'L0_gnn_b3': _L0_gnn_in['b3'], 'L1_gnn_W1': _L1_gnn_in['W1'], 'L1_gnn_att_src1': _L1_gnn_in['att_src1'], 'L1_gnn_att_dst1': _L1_gnn_in['att_dst1'], 'L1_gnn_b1': _L1_gnn_in['b1'], 'L1_gnn_W2': _L1_gnn_in['W2'], 'L1_gnn_att_src2': _L1_gnn_in['att_src2'], 'L1_gnn_att_dst2': _L1_gnn_in['att_dst2'], 'L1_gnn_b2': _L1_gnn_in['b2']}

def reference(x, src, dst, L0_gnn_W1, L0_gnn_b1, L0_gnn_W2, L0_gnn_b2, L0_gnn_W3, L0_gnn_b3, L1_gnn_W1, L1_gnn_att_src1, L1_gnn_att_dst1, L1_gnn_b1, L1_gnn_W2, L1_gnn_att_src2, L1_gnn_att_dst2, L1_gnn_b2):
    import jax
    import jax.numpy as jnp

    def _L0_gnn_ref(x, edge_index, W1, b1, W2, b2, W3, b3):
        import jax, jax.numpy as jnp
        import numpy as np
        N_NODES = 6250
        N_EDGES = 100000
        D_IN = 128
        U = 128
        H = 128
        h = x @ W1 + b1
        src = edge_index[0]
        dst = edge_index[1]
        h_i = h[dst]
        h_j = h[src]
        e = jnp.concatenate([h_i, h_j - h_i], axis=-1)
        m = jax.nn.relu(e @ W2 + b2)
        m = jax.nn.relu(m @ W3 + b3)
        out = jax.ops.segment_max(m, dst, num_segments=N_NODES)
        return jax.nn.relu(out)

    def _L1_gnn_ref(x, edge_index, W1, att_src1, att_dst1, b1, W2, att_src2, att_dst2, b2):
        import jax, jax.numpy as jnp
        import numpy as np
        NEG_SLOPE = 0.2

        def _gat_conv(x, W, att_src, att_dst, bias, src, dst, n_nodes):
            h = x @ W
            a_src = h @ att_src
            a_dst = h @ att_dst
            e = a_src[src] + a_dst[dst]
            e = jnp.where(e > 0, e, NEG_SLOPE * e)
            m = jax.ops.segment_max(e, dst, num_segments=n_nodes)
            ex = jnp.exp(e - m[dst])
            denom = jax.ops.segment_sum(ex, dst, num_segments=n_nodes)
            alpha = ex / denom[dst]
            msg = alpha[:, None] * h[src]
            out = jax.ops.segment_sum(msg, dst, num_segments=n_nodes)
            return out + bias
        n_nodes = x.shape[0]
        loops = jnp.arange(n_nodes, dtype=edge_index.dtype)
        src = jnp.concatenate([edge_index[0], loops])
        dst = jnp.concatenate([edge_index[1], loops])
        h = _gat_conv(x, W1, att_src1, att_dst1, b1, src, dst, n_nodes)
        h = jax.nn.relu(h)
        h = _gat_conv(h, W2, att_src2, att_dst2, b2, src, dst, n_nodes)
        return jax.nn.relu(h)
    edge_index = jnp.stack([src, dst])
    x = _layernorm(x + _L0_gnn_ref(x, edge_index, L0_gnn_W1, L0_gnn_b1, L0_gnn_W2, L0_gnn_b2, L0_gnn_W3, L0_gnn_b3), axis=-1)
    x = _layernorm(x + _L1_gnn_ref(x, edge_index, L1_gnn_W1, L1_gnn_att_src1, L1_gnn_att_dst1, L1_gnn_b1, L1_gnn_W2, L1_gnn_att_src2, L1_gnn_att_dst2, L1_gnn_b2), axis=-1)
    return x

_drawn_inputs = setup_inputs


def setup_inputs(seed=0):
    import zlib

    import numpy as np

    out = dict(_drawn_inputs(seed))
    spreads = {'L1_gnn_b1': (0.0, 0.1), 'L1_gnn_b2': (0.0, 0.1)}
    factors = {'L0_gnn_b1': 8.0,
     'L0_gnn_b2': 8.0,
     'L0_gnn_b3': 6.629,
     'L1_gnn_att_dst1': 8.0,
     'L1_gnn_att_src2': 5.759,
     'L1_gnn_att_dst2': 8.0}
    for name, (base, spread) in spreads.items():
        noise = np.random.default_rng([zlib.crc32(name.encode()), seed]).standard_normal(out[name].shape)
        drawn = base * np.exp(spread * noise) if base else spread * noise
        out[name] = jnp.asarray(drawn.astype(out[name].dtype))
    for name, factor in factors.items():
        out[name] = (out[name] * factor).astype(out[name].dtype)
    return out
```

```python
from contextlib import ExitStack

import concourse.bass as bass
from concourse import mybir
from concourse.alu_op_type import AluOpType as ALU

F32 = mybir.dt.float32
I32 = mybir.dt.int32
ACT = mybir.ActivationFunctionType
AX_X = mybir.AxisListType.X

P = 128
BIG = 1.0e30
SLOPE = 0.2
EPS = 1e-5
ROUND = 12582912.0


class Signal:

    def __init__(self, sem):
        self.sem, self.value = sem, 0

    def after(self, instruction, n=1):
        instruction.then_inc(self.sem, n)
        self.value += n
        return self.sem, self.value


def wait(engine, *marks):
    for sem, value in marks:
        engine.wait_ge(sem, value)


def edge_network(nc, t, out):
    N, F = t["x"].shape
    L = t["src"].shape[1]
    NB = -(-N // P)
    NP = NB * P
    CHUNKS = L
    FULL, REST = N // P, N % P
    G = 16
    RING = 3
    W = F + 2
    groups = [(j, min(j + G, L)) for j in range(0, L, G)]
    vector, scalar, tensor, pool, sync = nc.vector, nc.scalar, nc.tensor, nc.gpsimd, nc.sync

    P_table = nc.dram_tensor("P_table", (NP, F), F32).ap()
    Q_table = nc.dram_tensor("Q_table", (NP, F), F32).ap()
    H_table = nc.dram_tensor("H_table", (NP, W), F32).ap()
    run_max = nc.dram_tensor("run_max", (P * L, F), F32).ap()
    run_sum = nc.dram_tensor("run_sum", (P * L, W), F32).ap()
    carry_max = nc.dram_tensor("carry_max", (P, F), F32).ap()
    carry_sum = nc.dram_tensor("carry_sum", (P, W), F32).ap()
    ad_edges = nc.dram_tensor("ad_edges", (P * L, 1), F32).ap()

    with ExitStack() as ctx:
        def sb(name, shape, dt=F32):
            return ctx.enter_context(nc.sbuf_tensor(name, shape, dt))

        def signal(name):
            return Signal(ctx.enter_context(nc.semaphore(name)))

        def nodes(flat, width):
            return flat[:, 0:NB * width].rearrange("p (k f) -> p k f", f=width)

        ident, tri, ones = sb("ident", [P, P]), sb("tri", [P, P]), sb("ones", [P, P])
        shift, wrap, iota_row = sb("shift", [P, P]), sb("wrap", [P, P]), sb("iota_row", [P, P])
        iota_i = sb("iota_i", [P, P], I32)
        next_i, next_n = sb("next_i", [P, NB], I32), sb("next_n", [P, NB])
        x_sb = sb("x_sb", [P, NB, F])
        turned = sb("turned", [P, NP])
        tab = sb("tab", [P, NB, W])
        ring_a, ring_b = sb("ring_a", [P, NB * W]), sb("ring_b", [P, NB * W])
        src_i, dst_i = sb("src_i", [P, L], I32), sb("dst_i", [P, L], I32)
        neg, ad_exp = sb("neg", [P, L]), sb("ad_exp", [P, L])
        weights = {n: sb(n, [P, w]) for n, w in (
            ("W1", F), ("W2a", F), ("W2b", F), ("Wpq", 2 * F), ("W3", F), ("Wt", F))}
        conv_w = [sb(f"conv_w{c}", [P, W]) for c in range(2)]
        b1_col = sb("b1_col", [P, 1])
        att_cols = [sb(f"att{c}", [P, 2]) for c in range(2)]
        bias = {n: sb(n + "_rows", [P, F]) for n in ("b2", "b3", "c1", "c2")}
        NC13 = -(-CHUNKS // P)
        cf_i, cf_part = sb("cf_i", [P, NC13], I32), sb("cf_part", [P, 2, NC13], I32)
        cf_f = sb("cf_f", [P, 2, NC13])
        onehot = sb("onehot", [P, 2, P])
        small = {n: sb(n, [P, NB]) for n in (
            "cnt", "base", "cfle", "row_f", "ends", "starts", "empty", "negE", "negC", "s0", "s1", "s2", "s3",
            "mean", "rstd", "ad", "rmax", "mfin")}
        row_i, end_i, pe_i, start_i = (sb(n, [P, NB], I32) for n in ("row_i", "end_i", "pe_i", "start_i"))
        zero_tile = sb("zero_tile", [P, W])
        rows = {n: sb("r_" + n, [P, P]) for n in ("dfirst", "dlast", "link", "ra", "adl", "rs", "ma", "ms", "l", "cc")}
        state, state_shift = sb("state", [P, P]), sb("state_shift", [P, 3, P])
        carry_sb = sb("carry_sb", [P, W])
        dcol = sb("dcol", [P, 2])
        m1T = sb("m1T", [P, 2, 512])
        gz, gm, gd, gw = (sb(n, [P, G]) for n in ("gz", "gt", "gd", "gw"))
        gmm = sb("gmm", [P, 2, G + 1])
        ge, gc = sb("ge", [P, 2, G]), sb("gc", [P, 2, G])
        ad_first = sb("ad_first", [P, 1])
        ps = [ctx.enter_context(nc.psum_tensor(f"ps{i}", [P, 512], F32)) for i in range(8)]

        vec, act, pe, gp = signal("vec"), signal("act"), signal("pe"), signal("gp")
        loads = {n: signal("ld_" + n) for n in ("x", "w", "edges", "cf", "rows", "ad", "adx")}
        stores = {n: signal("st_" + n) for n in ("tabs", "h", "carry", "zero", "adscatter", "out", "run")}
        q_sem = [signal(f"q_slot{i}") for i in range(RING)]
        p_sem = [signal(f"p_slot{i}") for i in range(RING)]
        s_sem = [signal(f"s_slot{i}") for i in range(RING)]

        zeroed = gp.after(pool.memset(x_sb[:, NB - 1, :], 0.0))
        wait(sync, zeroed)
        x_in = t["x"][0:FULL * P, :].rearrange("(k p) f -> p k f", p=P)
        loads["x"].after(sync.dma_start(x_sb[:, 0:FULL, :], x_in), 16)
        x_ready = loads["x"].after(sync.dma_start(x_sb[0:REST, FULL, :], t["x"][FULL * P:N, :]), 16)
        ld = loads["w"]
        W2 = t["W2"]
        for dst, srcap in (
            (weights["W1"][:, :], t["W1"]), (weights["W2a"][:, :], W2[0:F, :]), (weights["W2b"][:, :], W2[F:2 * F, :]),
            (weights["W3"][:, :], t["W3"]), (conv_w[0][:, 0:F], t["C1"]), (conv_w[1][:, 0:F], t["C2"]),
            (b1_col[:, :], t["b1"].rearrange("(p a) -> p a", a=1)),
            (att_cols[0][:, 0:1], t["as1"].rearrange("(p a) -> p a", a=1)),
            (att_cols[0][:, 1:2], t["ad1"].rearrange("(p a) -> p a", a=1)),
            (att_cols[1][:, 0:1], t["as2"].rearrange("(p a) -> p a", a=1)),
            (att_cols[1][:, 1:2], t["ad2"].rearrange("(p a) -> p a", a=1)),
        ) + tuple((bias[n][:, :], t[k].rearrange("(a f) -> a f", a=1).broadcast_to([P, F]))
                  for n, k in (("b2", "b2"), ("b3", "b3"), ("c1", "cb1"), ("c2", "cb2"))):
            w_ready = ld.after(scalar.dma_start(dst, srcap), 16)
        loads["edges"].after(sync.dma_start(src_i[:, :], t["src"]), 16)
        edges_ready = loads["edges"].after(sync.dma_start(dst_i[:, :], t["dst"]), 16)
        flat_dst = t["dst"].rearrange("p l -> (p l)").rearrange("(c e) -> c e", e=P)
        padded = gp.after(pool.memset(cf_i[:, :], NP + P))
        wait(sync, padded)
        with nc.allow_non_contiguous_dma(reason="one value of every 128, once"):
            for k in range(NC13):
                n = min(P, CHUNKS - k * P)
                cf_ready = loads["cf"].after(sync.dma_start(cf_i[0:n, k:k + 1], flat_dst[k * P:k * P + n, 0:1]), 16)

        gp.after(pool.memset(ident[:, :], 0.0))
        gp.after(pool.memset(ones[:, :], 1.0))
        gp.after(pool.memset(tri[:, :], 1.0))
        gp.after(pool.memset(shift[:, :], 0.0))
        gp.after(pool.memset(zero_tile[:, :], 0.0))
        made = gp.after(pool.memset(wrap[:, :], 0.0))
        wait(pool, made)
        for m, op, fill, base, step, cm in ((ident, ALU.not_equal, 1.0, 0, -1, 1), (tri, ALU.is_ge, 0.0, 0, 1, -1),
                                            (shift, ALU.not_equal, 1.0, 1, -1, 1), (wrap, ALU.not_equal, 1.0, 1 - P, -1, 1)):
            gp.after(pool.affine_select(out=m[:, :], in_=m[:, :], compare_op=op, fill=fill, base=base,
                                        pattern=[[step, P]], channel_multiplier=cm))
        gp.after(pool.iota(iota_i[:, :], pattern=[[1, P]], base=0, channel_multiplier=0))
        consts = gp.after(pool.iota(next_i[:, :], pattern=[[P, NB]], base=1, channel_multiplier=1))

        wait(vector, consts, w_ready, cf_ready, edges_ready)
        vec.after(vector.tensor_copy(iota_row[:, :], iota_i[:, :]))
        vec.after(vector.tensor_copy(next_n[:, :], next_i[:, :]))
        vec.after(vector.tensor_tensor(weights["Wpq"][:, 0:F], weights["W2a"][:, :], weights["W2b"][:, :], ALU.subtract))
        folded = vec.after(vector.tensor_copy(weights["Wpq"][:, F:2 * F], weights["W2b"][:, :]))
        vec.after(vector.tensor_scalar(cf_part[:, 0, :], cf_i[:, :], P - 1, None, ALU.bitwise_and))
        m = vec.after(vector.tensor_scalar(cf_part[:, 1, :], cf_i[:, :], 7, None, ALU.logical_shift_right))
        wait(vector, m)
        m = vec.after(vector.tensor_copy(cf_f[:, :, :], cf_part[:, :, :]))
        m2 = vec.after(vector.tensor_tensor(neg[:, 1:L], dst_i[:, 1:L], dst_i[:, 0:L - 1], ALU.not_equal))
        vec.after(vector.memset(neg[:, 0:1], -BIG))
        wait(vector, m2)
        neg_ready = vec.after(vector.tensor_scalar(neg[:, 1:L], neg[:, 1:L], -BIG, None, ALU.mult))
        vec.after(vector.tensor_copy(dcol[:, 0:1], dst_i[:, 0:1]))
        dcol_ready = vec.after(vector.tensor_copy(dcol[:, 1:2], dst_i[:, L - 1:L]))

        used = None
        for k in range(NC13):
            wait(vector, m, *([used] if used else []))
            vec.after(vector.tensor_scalar(onehot[:, 0, :], iota_row[:, :], cf_f[:, 0, k:k + 1], None, ALU.is_equal))
            hot = vec.after(vector.tensor_scalar(onehot[:, 1, 0:NB], iota_row[:, 0:NB], cf_f[:, 1, k:k + 1], None, ALU.is_equal))
            wait(tensor, hot)
            used = pe.after(tensor.matmul(ps[0][:, 0:NB], lhsT=onehot[:, 0, :], rhs=onehot[:, 1, 0:NB],
                                          start=(k == 0), stop=(k == NC13 - 1)))
        wait(vector, used)
        m = vec.after(vector.tensor_copy(small["cnt"][:, :], ps[0][:, 0:NB]))
        wait(tensor, m)
        pe.after(tensor.matmul(ps[1][:, 0:NB], lhsT=tri[:, :], rhs=small["cnt"][:, :], start=True, stop=True))
        m = pe.after(tensor.matmul(ps[2][:, 0:NB], lhsT=ones[:, :], rhs=small["cnt"][:, :], start=True, stop=True))
        wait(vector, m)
        m = vec.after(vector.tensor_copy(small["s0"][:, :], ps[2][:, 0:NB]))
        wait(vector, m)
        m = vec.after(vector.tensor_tensor_scan(small["base"][:, :], ones[:, 0:NB], small["s0"][:, :], 0.0, ALU.mult, ALU.add))
        wait(vector, m)
        m = vec.after(vector.tensor_tensor(small["base"][:, :], small["base"][:, :], small["s0"][:, :], ALU.subtract))
        wait(vector, m)
        m = vec.after(vector.tensor_tensor(small["cfle"][:, :], ps[1][:, 0:NB], small["base"][:, :], ALU.add))
        wait(vector, m)
        m = vec.after(vector.tensor_scalar(small["row_f"][:, :], small["cfle"][:, :], -1.0, 0.0, ALU.add, ALU.max))
        wait(vector, m)
        m = vec.after(vector.tensor_copy(row_i[:, :], small["row_f"][:, :]))
        wait(pool, m)
        dst_rows = ring_a[:, :].bitcast(I32)[:, 0:NP].rearrange("p (k e) -> p k e", e=P)
        for k in range(NB):
            m = loads["rows"].after(pool.indirect_dma_start(
                out=dst_rows[:, k, :], out_offset=None, in_=flat_dst,
                in_offset=bass.IndirectOffsetOnAxis(ap=row_i[:, k:k + 1], axis=0)), 16)
        wait(vector, m)
        below = nodes(ring_b, P)
        m = vec.after(vector.tensor_tensor(below, dst_rows, next_n[:, :].unsqueeze(2).to_broadcast([P, NB, P]), ALU.is_lt))
        wait(vector, m)
        m = vec.after(vector.tensor_reduce(small["s0"][:, :], below, AX_X, ALU.add))
        wait(vector, m)
        m = ends_ready = vec.after(vector.scalar_tensor_tensor(out=small["ends"][:, :], in0=small["row_f"][:, :], scalar=float(P),
                                                  in1=small["s0"][:, :], op0=ALU.mult, op1=ALU.add))
        rows_free = m
        wait(tensor, m)
        tensor.matmul(ps[1][:, 0:NB], lhsT=shift[:, :], rhs=small["ends"][:, :], start=True, stop=False)
        m = pe.after(tensor.matmul(ps[1][:, 1:NB], lhsT=wrap[:, :], rhs=small["ends"][:, 0:NB - 1], start=False, stop=True))
        wait(vector, m)
        m = vec.after(vector.tensor_copy(small["starts"][:, :], ps[1][:, 0:NB]))
        wait(vector, m)
        s = small

        def chain(instructions):
            mark = None
            for make in instructions:
                mark = vec.after(make())
                wait(vector, mark)
            return mark

        index_ready = chain([
            lambda: vector.tensor_tensor(s["empty"][:, :], s["ends"][:, :], s["starts"][:, :], ALU.is_equal),
            lambda: vector.tensor_scalar(s["negE"][:, :], s["empty"][:, :], -BIG, None, ALU.mult),
            lambda: vector.scalar_tensor_tensor(out=s["s0"][:, :], in0=s["empty"][:, :], scalar=1.0e6, in1=s["starts"][:, :],
                                                op0=ALU.mult, op1=ALU.add),
            lambda: vector.tensor_copy(start_i[:, :], s["s0"][:, :]),
            lambda: vector.tensor_scalar(s["s0"][:, :], s["ends"][:, :], -1.0, 0.0, ALU.add, ALU.max),
            lambda: vector.tensor_copy(end_i[:, :], s["s0"][:, :]),
            lambda: vector.tensor_scalar(s["s1"][:, :], s["s0"][:, :], 0.5, 1.0 / L, ALU.add, ALU.mult),
            lambda: vector.tensor_scalar(s["s1"][:, :], s["s1"][:, :], -0.5, ROUND, ALU.add, ALU.add),
            lambda: vector.tensor_scalar(s["s1"][:, :], s["s1"][:, :], -ROUND, None, ALU.add),
            lambda: vector.tensor_copy(pe_i[:, :], s["s1"][:, :]),
            lambda: vector.scalar_tensor_tensor(out=s["s0"][:, :], in0=s["s1"][:, :], scalar=float(L), in1=s["starts"][:, :],
                                                op0=ALU.mult, op1=ALU.is_le),
            lambda: vector.tensor_scalar(s["negC"][:, :], s["s0"][:, :], -BIG, None, ALU.mult),
        ])

        def spread(column, bank):
            return pe.after(tensor.matmul(bank, lhsT=column.to_broadcast([P, P]), rhs=ident[:, :], start=True, stop=True))

        wait(tensor, dcol_ready, index_ready)
        spread(dcol[:, 0:1], ps[0][:, 0:P])
        m = spread(dcol[:, 1:2], ps[1][:, 0:P])
        wait(vector, m)
        r = rows
        vec.after(vector.tensor_copy(r["dfirst"][:, :], ps[0][:, 0:P]))
        chain([
            lambda: vector.tensor_copy(r["dlast"][:, :], ps[1][:, 0:P]),
            lambda: vector.memset(r["link"][:, :], 0.0),
            lambda: vector.tensor_tensor(r["link"][:, 1:P], r["dfirst"][:, 1:P], r["dlast"][:, 0:P - 1], ALU.is_equal),
            lambda: vector.tensor_tensor(r["cc"][:, :], r["dfirst"][:, :], r["dlast"][:, :], ALU.is_equal),
            lambda: vector.tensor_tensor(r["link"][:, :], r["link"][:, :], r["cc"][:, :], ALU.mult),
        ])
        link_ready = chain([lambda: vector.tensor_scalar(r["link"][:, :], r["link"][:, :], -1.0, BIG, ALU.add, ALU.mult)])

        def turn(source, ready):
            wait(tensor, ready)
            free = {}
            for q, k0 in enumerate(range(0, NB, 4)):
                bank, ks = ps[6 + q % 2], range(k0, min(k0 + 4, NB))
                if q % 2 in free:
                    wait(tensor, free[q % 2])
                for k in ks:
                    mark = pe.after(tensor.transpose(bank[:, (k - k0) * P:(k - k0 + 1) * P], source[:, k, 0:F], ident[:, :]))
                wait(scalar, mark)
                n = len(ks) * P
                free[q % 2] = act.after(scalar.activation(turned[:, k0 * P:k0 * P + n], bank[:, 0:n], ACT.Copy))
            return free[q % 2]

        turned_x = turn(x_sb, x_ready)
        wait(tensor, w_ready, turned_x)
        free = {}
        for q, c0 in enumerate(range(0, NP, 512)):
            n = min(512, NP - c0)
            b = 2 + q % 2
            if b in free:
                wait(tensor, free[b])
            mark = pe.after(tensor.matmul(ps[b][:, 0:n], lhsT=weights["W1"][:, :], rhs=turned[:, c0:c0 + n], start=True, stop=True))
            wait(scalar, mark)
            free[b] = act.after(scalar.activation(turned[:, c0:c0 + n], ps[b][:, 0:n], ACT.Identity, bias=b1_col[:, 0:1]))
        h_ready = free[b]
        wait(tensor, h_ready, folded)
        wait(vector, rows_free)
        p_stage, q_stage = nodes(ring_a, F), nodes(ring_b, F)
        free = {}
        for q, k0 in enumerate(range(0, NB, 2)):
            ks = range(k0, min(k0 + 2, NB))
            b = 4 + q % 2
            if b in free:
                wait(tensor, free[b])
            for i, k in enumerate(ks):
                mark = pe.after(tensor.matmul(ps[b][:, i * 256:(i + 1) * 256], lhsT=turned[:, k * P:(k + 1) * P],
                                              rhs=weights["Wpq"][:, :], start=True, stop=True))
            wait(vector, mark)
            n = len(ks)
            both = ps[b][:, 0:n * 256].rearrange("p (k s f) -> p k s f", s=2, f=F)
            vec.after(vector.tensor_tensor(p_stage[:, k0:k0 + n, :], both[:, :, 0, :],
                                           bias["b2"][:, :].unsqueeze(1).to_broadcast([P, n, F]), ALU.add))
            free[b] = vec.after(vector.tensor_copy(q_stage[:, k0:k0 + n, :], both[:, :, 1, :]))
        wait(sync, free[b])
        stores["tabs"].after(sync.dma_start(P_table.rearrange("(k p) f -> p k f", p=P), p_stage), 16)
        tables_stored = stores["tabs"].after(sync.dma_start(Q_table.rearrange("(k p) f -> p k f", p=P), q_stage), 16)

        q_ring = ring_a[:, 0:RING * G * F].rearrange("p (s g f) -> p s g f", s=RING, f=F)
        p_ring = turned[:, 0:RING * G * F].rearrange("p (s g f) -> p s g f", s=RING, f=F)
        r_ring = ring_b[:, 0:RING * G * F].rearrange("p (s g f) -> p s g f", s=RING, f=F)
        wait(pool, tables_stored)
        wait(vector, tables_stored)
        q_free, s_stored, relu_free, z_free = {}, {}, {}, {}
        previous = zero_tile[:, 0:F]
        quad = 0
        for g, (j0, j1) in enumerate(groups):
            slot, n = g % RING, j1 - j0
            if slot in q_free:
                wait(pool, q_free[slot])
            for j in range(j0, j1):
                for ring, sems, table, idx in ((q_ring, q_sem, Q_table, src_i), (p_ring, p_sem, P_table, dst_i)):
                    got = sems[slot].after(pool.indirect_dma_start(
                        out=ring[:, slot, j - j0, :], out_offset=None, in_=table,
                        in_offset=bass.IndirectOffsetOnAxis(ap=idx[:, j:j + 1], axis=0)), 16)
            wait(vector, (q_sem[slot].sem, q_sem[slot].value), (p_sem[slot].sem, p_sem[slot].value))
            summed = vec.after(vector.tensor_tensor(q_ring[:, slot, 0:n, :], q_ring[:, slot, 0:n, :], p_ring[:, slot, 0:n, :], ALU.add))
            if slot in s_stored:
                wait(vector, s_stored[slot])
            wait(tensor, summed)
            for a in range(0, n, 4):
                m4 = min(4, n - a)
                b = quad % 2
                quad += 1
                if b in relu_free:
                    wait(tensor, relu_free[b])
                for i in range(m4):
                    mark = pe.after(tensor.transpose(ps[b][:, i * P:(i + 1) * P], q_ring[:, slot, a + i, :], ident[:, :]))
                wait(scalar, mark)
                if b in z_free:
                    wait(scalar, z_free[b][1])
                relu_free[b] = act.after(scalar.activation(m1T[:, b, 0:m4 * P], ps[b][:, 0:m4 * P], ACT.Relu))
                wait(tensor, relu_free[b])
                if b in z_free:
                    wait(tensor, z_free[b][0])
                for i in range(m4):
                    z_done = pe.after(tensor.matmul(ps[2 + b][:, i * P:(i + 1) * P], lhsT=m1T[:, b, i * P:(i + 1) * P],
                                                    rhs=weights["W3"][:, :], start=True, stop=True))
                wait(vector, z_done)
                for i in range(m4):
                    j = j0 + a + i
                    mark = vec.after(vector.scalar_tensor_tensor(
                        out=r_ring[:, slot, a + i, :], in0=previous, scalar=neg[:, j:j + 1],
                        in1=ps[2 + b][:, i * P:(i + 1) * P], op0=ALU.add, op1=ALU.max))
                    wait(vector, mark)
                    previous = r_ring[:, slot, a + i, :]
                z_free[b] = (mark, z_done)
            q_free[slot] = mark
            wait(sync, mark)
            s_stored[slot] = s_sem[slot].after(sync.dma_start(
                run_max.rearrange("(p l) f -> p l f", p=P)[:, j0:j1, :], r_ring[:, slot, 0:n, :]), 16)

        wait(tensor, mark)
        m = pe.after(tensor.transpose(ps[4][:, 0:P], previous, ident[:, :]))
        wait(vector, m)
        m = vec.after(vector.tensor_tensor_scan(state[:, :], r["link"][:, :], ps[4][:, 0:P], -BIG, ALU.add, ALU.max))
        wait(vector, m)
        vec.after(vector.memset(state_shift[:, 0, 0:1], 0.0))
        m = vec.after(vector.tensor_copy(state_shift[:, 0, 1:P], state[:, 0:P - 1]))
        wait(tensor, m)
        m = pe.after(tensor.transpose(ps[5][:, 0:P], state_shift[:, 0, :], ident[:, :]))
        wait(vector, m)
        m = vec.after(vector.tensor_copy(carry_sb[:, 0:F], ps[5][:, 0:P]))
        wait(sync, m)
        carried = stores["carry"].after(sync.dma_start(carry_max, carry_sb[:, 0:F]), 16)

        def gather_nodes(table, index, view, mark_sig):
            for k in range(NB):
                mark = mark_sig.after(pool.indirect_dma_start(
                    out=view[:, k, :], out_offset=None, in_=table,
                    in_offset=bass.IndirectOffsetOnAxis(ap=index[:, k:k + 1], axis=0)), 16)
            return mark

        def over(small_ap, width):
            return small_ap.unsqueeze(2).to_broadcast([P, NB, width])

        E, C = nodes(ring_a, F), nodes(ring_b, F)
        wait(pool, carried, *s_stored.values(), mark)
        gather_nodes(run_max, end_i, E, loads["rows"])
        m = gather_nodes(carry_max, pe_i, C, loads["rows"])
        wait(vector, m)
        chain([
            lambda: vector.tensor_tensor(E, E, over(s["negE"][:, :], F), ALU.add),
            lambda: vector.tensor_tensor(C, C, over(s["negC"][:, :], F), ALU.add),
            lambda: vector.tensor_tensor(E, E, C, ALU.max),
            lambda: vector.tensor_tensor(E, E, bias["b3"][:, :].unsqueeze(1).to_broadcast([P, NB, F]), ALU.add),
            lambda: vector.tensor_scalar(E, E, 0.0, None, ALU.max),
            lambda: vector.tensor_tensor(x_sb[:, :, :], x_sb[:, :, :], E, ALU.add),
        ])

        def layernorm(y, squares):
            chain([
                lambda: vector.tensor_reduce(s["mean"][:, :], y, AX_X, ALU.add),
                lambda: vector.tensor_scalar(s["mean"][:, :], s["mean"][:, :], 1.0 / F, None, ALU.mult),
                lambda: vector.tensor_tensor(y, y, over(s["mean"][:, :], F), ALU.subtract),
                lambda: vector.tensor_tensor(squares, y, y, ALU.mult),
                lambda: vector.tensor_reduce(s["rstd"][:, :], squares, AX_X, ALU.add),
            ])
            m = chain([lambda: vector.tensor_scalar(s["rstd"][:, :], s["rstd"][:, :], 1.0 / F, EPS, ALU.mult, ALU.add)])
            wait(scalar, m)
            m = act.after(scalar.activation(s["rstd"][:, :], s["rstd"][:, :], ACT.Sqrt))
            wait(vector, m)
            return chain([
                lambda: vector.reciprocal(s["rstd"][:, :], s["rstd"][:, :]),
                lambda: vector.tensor_tensor(y, y, over(s["rstd"][:, :], F), ALU.mult),
            ])

        x1_ready = layernorm(x_sb[:, :, :], nodes(ring_a, F))

        wait(sync, x1_ready)
        zeros = ring_b[:, 0:L]
        m = vec.after(vector.memset(zeros, 0.0))
        wait(sync, m)
        zero_stored = stores["zero"].after(sync.dma_start(ad_edges.rearrange("(p l) a -> p (l a)", p=P), zeros), 16)

        source, ready = x_sb[:, :, :], x1_ready
        for layer in range(2):
            w = conv_w[layer]
            wait(tensor, ready)
            m = pe.after(tensor.transpose(ps[6][:, 0:P], w[:, 0:F], ident[:, :]))
            wait(vector, m)
            m = vec.after(vector.tensor_copy(weights["Wt"][:, :], ps[6][:, 0:P]))
            wait(tensor, m)
            m = pe.after(tensor.matmul(ps[7][:, 0:2], lhsT=weights["Wt"][:, :], rhs=att_cols[layer][:, :], start=True, stop=True))
            wait(vector, m)
            w_made = vec.after(vector.tensor_copy(w[:, F:W], ps[7][:, 0:2]))
            wait(tensor, w_made)
            src_turned = turn(source, ready)
            wait(tensor, src_turned)
            free = {}
            for q, k0 in enumerate(range(0, NB, 3)):
                n = min(3, NB - k0)
                b = 2 + q % 2
                if b in free:
                    wait(tensor, free[b])
                for i in range(n):
                    mark = pe.after(tensor.matmul(ps[b][:, i * W:(i + 1) * W], lhsT=turned[:, (k0 + i) * P:(k0 + i + 1) * P],
                                                  rhs=w[:, :], start=True, stop=True))
                wait(vector, mark)
                blk = ps[b][:, 0:n * W].rearrange("p (k f) -> p k f", f=W)
                vec.after(vector.tensor_copy(tab[:, k0:k0 + n, 0:F], blk[:, :, 0:F]))
                vec.after(vector.tensor_copy(tab[:, k0:k0 + n, F + 1], blk[:, :, F]))
                free[b] = vec.after(vector.tensor_copy(s["ad"][:, k0:k0 + n], blk[:, :, F + 1]))
            tab_ready = vec.after(vector.memset(tab[:, :, F:F + 1], 1.0))
            wait(sync, tab_ready)
            h_stored = stores["h"].after(sync.dma_start(H_table.rearrange("(k p) f -> p k f", p=P), tab[:, :, :]), 16)

            wait(pool, tab_ready, zero_stored)
            for k in range(NB):
                m = stores["adscatter"].after(pool.indirect_dma_start(
                    out=ad_edges, out_offset=bass.IndirectOffsetOnAxis(ap=start_i[:, k:k + 1], axis=0),
                    in_=s["ad"][:, k:k + 1], in_offset=None, bounds_check=P * L - 1, oob_is_err=False), 16)
            wait(sync, m)
            m = loads["ad"].after(sync.dma_start(ad_exp[:, :], ad_edges.rearrange("(p l) a -> p (l a)", p=P)), 16)
            wait(vector, m)
            with nc.allow_non_contiguous_dma(reason="one column, once a layer"):
                wait(sync, tab_ready)
                adn = nc.dram_tensor(f"ad_nodes{layer}", (NP, 1), F32).ap()
                m2 = stores["h"].after(sync.dma_start(adn.rearrange("(k p) a -> p k a", p=P), s["ad"][:, :].unsqueeze(2)), 16)
            wait(pool, m2)
            m2 = loads["adx"].after(pool.indirect_dma_start(out=ad_first[:, :], out_offset=None, in_=adn,
                                    in_offset=bass.IndirectOffsetOnAxis(ap=dst_i[:, 0:1], axis=0)), 16)
            wait(vector, m2)
            keep = ring_b[:, 0:L]
            ad_ready = chain([
                lambda: vector.tensor_scalar(keep, neg[:, :], 0.0, None, ALU.is_ge),
                lambda: vector.tensor_copy(ad_exp[:, 0:1], ad_first[:, :]),
                lambda: vector.tensor_tensor_scan(ring_b[:, L:2 * L], keep, ad_exp[:, :], 0.0, ALU.mult, ALU.add),
                lambda: vector.tensor_copy(ad_exp[:, :], ring_b[:, L:2 * L]),
            ])

            h_ring = ring_a[:, 0:RING * G * W].rearrange("p (s g f) -> p s g f", s=RING, f=W)
            r_ring = ring_b[:, 0:RING * G * W].rearrange("p (s g f) -> p s g f", s=RING, f=W)
            wait(pool, h_stored, src_turned)
            h_free, s_stored, w_used = {}, {}, {}
            previous, prev_max = zero_tile[:, 0:F + 1], zero_tile[:, F + 1:W]
            m = vec.after(vector.memset(gmm[:, 1, G:G + 1], 0.0))
            wait(vector, m)
            last = m
            pn = G
            for g, (j0, j1) in enumerate(groups):
                slot, n, par = g % RING, j1 - j0, g % 2
                if slot in h_free:
                    wait(pool, h_free[slot])
                for j in range(j0, j1):
                    got = q_sem[slot].after(pool.indirect_dma_start(
                        out=h_ring[:, slot, j - j0, :], out_offset=None, in_=H_table,
                        in_offset=bass.IndirectOffsetOnAxis(ap=src_i[:, j:j + 1], axis=0)), 16)
                wait(vector, got)
                if slot in s_stored:
                    wait(vector, s_stored[slot])
                a_src = h_ring[:, slot, 0:n, F + 1]
                top = r_ring[:, slot, 0:n, F + 1]
                ngs, ads = neg[:, j0:j1], ad_exp[:, j0:j1]
                m = vec.after(vector.tensor_tensor_scan(top, ngs, a_src, prev_max, ALU.add, ALU.max))
                m2 = vec.after(vector.tensor_tensor(gz[:, 0:n], a_src, ads, ALU.add))
                wait(vector, m)
                m3 = vec.after(vector.tensor_tensor(gd[:, 0:n], top, ads, ALU.add))
                wait(vector, m3)
                mm = gmm[:, par, :]
                m = vec.after(vector.scalar_tensor_tensor(out=mm[:, 1:n + 1], in0=gd[:, 0:n], scalar=SLOPE, in1=gd[:, 0:n],
                                                          op0=ALU.mult, op1=ALU.max))
                vec.after(vector.tensor_copy(mm[:, 0:1], gmm[:, 1 - par, pn:pn + 1]))
                m2 = vec.after(vector.scalar_tensor_tensor(out=gw[:, 0:n], in0=gz[:, 0:n], scalar=SLOPE, in1=gz[:, 0:n],
                                                           op0=ALU.mult, op1=ALU.max))
                wait(vector, m2)
                if par in w_used:
                    wait(vector, w_used[par])
                vec.after(vector.tensor_tensor(ge[:, par, 0:n], gw[:, 0:n], mm[:, 1:n + 1], ALU.subtract))
                m = vec.after(vector.tensor_tensor(gz[:, 0:n], mm[:, 0:n], mm[:, 1:n + 1], ALU.subtract))
                wait(vector, m)
                m = vec.after(vector.tensor_tensor(gc[:, par, 0:n], gz[:, 0:n], ngs, ALU.add))
                wait(scalar, m)
                act.after(scalar.activation(ge[:, par, 0:n], ge[:, par, 0:n], ACT.Exp))
                m = act.after(scalar.activation(gc[:, par, 0:n], gc[:, par, 0:n], ACT.Exp))
                wait(scalar, m)
                wait(vector, m)
                for i in range(n):
                    scaled = act.after(scalar.activation(h_ring[:, slot, i, 0:F + 1], h_ring[:, slot, i, 0:F + 1], ACT.Copy,
                                                         scale=ge[:, par, i:i + 1]))
                    wait(vector, scaled)
                    last = vec.after(vector.scalar_tensor_tensor(
                        out=r_ring[:, slot, i, 0:F + 1], in0=previous, scalar=gc[:, par, i:i + 1],
                        in1=h_ring[:, slot, i, 0:F + 1], op0=ALU.mult, op1=ALU.add))
                    wait(vector, last)
                    previous = r_ring[:, slot, i, 0:F + 1]
                prev_max = r_ring[:, slot, n - 1, F + 1:W]
                whole_last = r_ring[:, slot, n - 1, :]
                pn = n
                w_used[par] = scaled
                h_free[slot] = last
                wait(sync, last)
                s_stored[slot] = s_sem[slot].after(sync.dma_start(
                    run_sum.rearrange("(p l) f -> p l f", p=P)[:, j0:j1, :], r_ring[:, slot, 0:n, :]), 16)

            wait(tensor, last)
            pe.after(tensor.transpose(ps[4][:, 0:P], whole_last[:, 0:F], ident[:, :]))
            spread(whole_last[:, F + 1:W], ps[5][:, 0:P])
            spread(ad_exp[:, L - 1:L], ps[6][:, 0:P])
            m = spread(whole_last[:, F:F + 1], ps[7][:, 0:P])
            wait(vector, m)
            m = chain([
                lambda: vector.tensor_copy(r["ra"][:, :], ps[5][:, 0:P]),
                lambda: vector.tensor_copy(r["adl"][:, :], ps[6][:, 0:P]),
                lambda: vector.tensor_tensor_scan(r["rs"][:, :], r["link"][:, :], r["ra"][:, :], -BIG, ALU.add, ALU.max),
                lambda: vector.tensor_tensor(r["ma"][:, :], r["ra"][:, :], r["adl"][:, :], ALU.add),
                lambda: vector.scalar_tensor_tensor(out=r["ma"][:, :], in0=r["ma"][:, :], scalar=SLOPE, in1=r["ma"][:, :], op0=ALU.mult, op1=ALU.max),
                lambda: vector.tensor_tensor(r["ms"][:, :], r["rs"][:, :], r["adl"][:, :], ALU.add),
                lambda: vector.scalar_tensor_tensor(out=r["ms"][:, :], in0=r["ms"][:, :], scalar=SLOPE, in1=r["ms"][:, :], op0=ALU.mult, op1=ALU.max),
                lambda: vector.tensor_tensor(r["ma"][:, :], r["ma"][:, :], r["ms"][:, :], ALU.subtract),
                lambda: vector.memset(r["cc"][:, :], 0.0),
                lambda: vector.tensor_tensor(r["cc"][:, 1:P], r["ms"][:, 0:P - 1], r["ms"][:, 1:P], ALU.subtract),
                lambda: vector.tensor_tensor(r["cc"][:, :], r["cc"][:, :], r["link"][:, :], ALU.add),
            ])
            wait(scalar, m)
            act.after(scalar.activation(r["ma"][:, :], r["ma"][:, :], ACT.Exp))
            m = act.after(scalar.activation(r["cc"][:, :], r["cc"][:, :], ACT.Exp))
            wait(vector, m)
            m = chain([
                lambda: vector.tensor_tensor(r["l"][:, :], ps[7][:, 0:P], r["ma"][:, :], ALU.mult),
                lambda: vector.tensor_tensor(r["ma"][:, :], ps[4][:, 0:P], r["ma"][:, :], ALU.mult),
                lambda: vector.memset(state_shift[:, :, :], 0.0),
                lambda: vector.tensor_tensor_scan(state[:, :], r["cc"][:, :], r["ma"][:, :], 0.0, ALU.mult, ALU.add),
                lambda: vector.tensor_copy(state_shift[:, 0, 1:P], state[:, 0:P - 1]),
                lambda: vector.tensor_tensor_scan(state[:, :], r["cc"][:, :], r["l"][:, :], 0.0, ALU.mult, ALU.add),
                lambda: vector.tensor_copy(state_shift[:, 1, 1:P], state[:, 0:P - 1]),
                lambda: vector.tensor_copy(state_shift[:, 2, 1:P], r["rs"][:, 0:P - 1]),
            ])
            wait(tensor, m)
            for i in range(3):
                m = pe.after(tensor.transpose(ps[4 + i][:, 0:P], state_shift[:, i, :], ident[:, :]))
            wait(vector, m)
            m = chain([
                lambda: vector.tensor_copy(carry_sb[:, 0:F], ps[4][:, 0:P]),
                lambda: vector.tensor_copy(carry_sb[:, F:F + 1], ps[5][:, 0:1]),
                lambda: vector.tensor_copy(carry_sb[:, F + 1:W], ps[6][:, 0:1]),
            ])
            wait(sync, m)
            carried = stores["carry"].after(sync.dma_start(carry_sum, carry_sb[:, :]), 16)

            E, C = nodes(ring_a, W), nodes(ring_b, W)
            wait(pool, carried, *s_stored.values(), last)
            gather_nodes(run_sum, end_i, E, loads["rows"])
            m = gather_nodes(carry_sum, pe_i, C, loads["rows"])
            wait(vector, m)

            def leaky_sum(o, a, b):
                return [lambda: vector.tensor_tensor(o, a, b, ALU.add),
                        lambda: vector.scalar_tensor_tensor(out=o, in0=o, scalar=SLOPE, in1=o, op0=ALU.mult, op1=ALU.max)]

            ad_n = s["ad"][:, :]
            m = chain([
                lambda: vector.tensor_tensor(s["s0"][:, :], E[:, :, F + 1], s["negE"][:, :], ALU.add),
                lambda: vector.tensor_tensor(s["s1"][:, :], C[:, :, F + 1], s["negC"][:, :], ALU.add),
                lambda: vector.tensor_tensor(s["rmax"][:, :], s["s0"][:, :], s["s1"][:, :], ALU.max),
                lambda: vector.tensor_tensor(s["rmax"][:, :], s["rmax"][:, :], tab[:, :, F + 1], ALU.max),
            ] + leaky_sum(s["mfin"][:, :], s["rmax"][:, :], ad_n) + leaky_sum(s["s0"][:, :], s["s0"][:, :], ad_n)
              + leaky_sum(s["s1"][:, :], s["s1"][:, :], ad_n) + leaky_sum(s["s2"][:, :], tab[:, :, F + 1], ad_n) + [
                lambda: vector.tensor_tensor(s["s0"][:, :], s["s0"][:, :], s["mfin"][:, :], ALU.subtract),
                lambda: vector.tensor_tensor(s["s1"][:, :], s["s1"][:, :], s["mfin"][:, :], ALU.subtract),
                lambda: vector.tensor_tensor(s["s2"][:, :], s["s2"][:, :], s["mfin"][:, :], ALU.subtract),
            ])
            wait(scalar, m)
            for n in ("s0", "s1", "s2"):
                m = act.after(scalar.activation(s[n][:, :], s[n][:, :], ACT.Exp))
            wait(vector, m)
            Ev, Cv, Tv = E[:, :, 0:F + 1], C[:, :, 0:F + 1], tab[:, :, 0:F + 1]
            name = "c1" if layer == 0 else "c2"
            ready = chain([
                lambda: vector.tensor_tensor(Ev, Ev, over(s["s0"][:, :], F + 1), ALU.mult),
                lambda: vector.tensor_tensor(Cv, Cv, over(s["s1"][:, :], F + 1), ALU.mult),
                lambda: vector.tensor_tensor(Ev, Ev, Cv, ALU.add),
                lambda: vector.tensor_tensor(Tv, Tv, over(s["s2"][:, :], F + 1), ALU.mult),
                lambda: vector.tensor_tensor(Ev, Ev, Tv, ALU.add),
                lambda: vector.reciprocal(s["s3"][:, :], E[:, :, F]),
                lambda: vector.tensor_tensor(E[:, :, 0:F], E[:, :, 0:F], over(s["s3"][:, :], F), ALU.mult),
                lambda: vector.tensor_tensor(E[:, :, 0:F], E[:, :, 0:F], bias[name][:, :].unsqueeze(1).to_broadcast([P, NB, F]), ALU.add),
                lambda: vector.tensor_scalar(E[:, :, 0:F], E[:, :, 0:F], 0.0, None, ALU.max),
            ])
            wait(vector, h_stored)
            source = E

        m = vec.after(vector.tensor_tensor(x_sb[:, :, :], x_sb[:, :, :], E[:, :, 0:F], ALU.add))
        wait(vector, m)
        m = layernorm(x_sb[:, :, :], nodes(ring_b, F))
        wait(sync, m)
        stores["out"].after(sync.dma_start(out[0:FULL * P, :].rearrange("(k p) f -> p k f", p=P), x_sb[:, 0:FULL, :]), 16)
        m = stores["out"].after(sync.dma_start(out[FULL * P:N, :], x_sb[0:REST, FULL, :]), 16)
        wait(sync, m)


_NAMES = {"x": "x", "src": "src", "dst": "dst", "W1": "L0_gnn_W1", "b1": "L0_gnn_b1", "W2": "L0_gnn_W2",
          "b2": "L0_gnn_b2", "W3": "L0_gnn_W3", "b3": "L0_gnn_b3", "C1": "L1_gnn_W1", "as1": "L1_gnn_att_src1",
          "ad1": "L1_gnn_att_dst1", "cb1": "L1_gnn_b1", "C2": "L1_gnn_W2", "as2": "L1_gnn_att_src2",
          "ad2": "L1_gnn_att_dst2", "cb2": "L1_gnn_b2"}


def kernel(**inputs):
    import numpy as np
    import concourse.bacc as bacc
    from concourse.bass_utils import run_bass_kernel_spmd

    N, F = inputs["x"].shape
    E = inputs["src"].shape[0]
    L = -(-E // 128)
    nc = bacc.Bacc("TRN2", target_bir_lowering=False, num_devices=1)
    arrays, aps = {}, {}
    for short, name in _NAMES.items():
        a = np.ascontiguousarray(inputs[name])
        if short in ("src", "dst"):
            a = np.concatenate([a, np.full(128 * L - E, 0 if short == "src" else N, a.dtype)]).reshape(128, L)
        arrays[f"in_{short}"] = a
        aps[short] = nc.dram_tensor(f"in_{short}", a.shape, mybir.dt.from_np(a.dtype), kind="ExternalInput").ap()
    out = nc.dram_tensor("out", (N, F), F32, kind="ExternalOutput").ap()
    edge_network(nc, aps, out)
    result = run_bass_kernel_spmd(nc, [arrays], core_ids=[0])
    return result.results[0]["out"]
```

```python
from contextlib import ExitStack

import concourse.bass as bass
from concourse import mybir
from concourse.alu_op_type import AluOpType as ALU

F32 = mybir.dt.float32
I32 = mybir.dt.int32
BF16 = mybir.dt.bfloat16
ACT = mybir.ActivationFunctionType
AX_X = mybir.AxisListType.X

P = 128
BIG = 1.0e30
SLOPE = 0.2
EPS = 1e-5
ROUND = 12582912.0


class Signal:

    def __init__(self, sem):
        self.sem, self.value = sem, 0

    def after(self, instruction, n=1):
        instruction.then_inc(self.sem, n)
        self.value += n
        return self.sem, self.value


def wait(engine, *marks):
    for sem, value in marks:
        engine.wait_ge(sem, value)


def edge_network(nc, t, out):
    N, F = t["x"].shape
    L = t["src"].shape[1]
    NB = -(-N // P)
    NP = NB * P
    CHUNKS = L
    FULL, REST = N // P, N % P
    G = 16
    RING = 3
    G1, RING1 = 14, 3
    PIECE = 4
    W = F + 2
    batches = [(k, min(k + 7, NB)) for k in range(0, NB, 7)]
    groups = [(j, min(j + G, L)) for j in range(0, L, G)]
    groups1 = [(j, min(j + G1, L)) for j in range(0, L, G1)]
    vector, scalar, tensor, pool, sync = nc.vector, nc.scalar, nc.tensor, nc.gpsimd, nc.sync

    CB = -(-CHUNKS // P)
    BL = CB * P
    WINDOWS = NP + P
    P_compact = nc.dram_tensor("P_compact", (WINDOWS, F), F32).ap()
    rank_rows = nc.dram_tensor("rank_rows", (2, P * BL), BF16).ap()
    first_ranks = nc.dram_tensor("first_ranks", (1, P * CB), I32).ap()
    Q_table = nc.dram_tensor("Q_table", (NP, F), F32).ap()
    H_table = nc.dram_tensor("H_table", (NP, W), F32).ap()
    run_max = nc.dram_tensor("run_max", (P * L, F), F32).ap()
    WR = 3
    run_sum = nc.dram_tensor("run_sum", (P * L, W), F32).ap()
    bounds_table = nc.dram_tensor("bounds_table", (NP, 2), F32).ap()
    ad_edges = nc.dram_tensor("ad_edges", (P * L, 1), F32).ap()

    with ExitStack() as ctx:
        def sb(name, shape, dt=F32):
            return ctx.enter_context(nc.sbuf_tensor(name, shape, dt))

        def signal(name):
            return Signal(ctx.enter_context(nc.semaphore(name)))

        def nodes(flat, width):
            return flat[:, 0:NB * width].rearrange("p (k f) -> p k f", f=width)

        ident, tri, ones = sb("ident", [P, P]), sb("tri", [P, P]), sb("ones", [P, P])
        shift, wrap, iota_row = sb("shift", [P, P]), sb("wrap", [P, P]), sb("iota_row", [P, P])
        iota_i, iota_col_i = sb("iota_i", [P, P], I32), sb("iota_col_i", [P, 1], I32)
        next_i, next_n = sb("next_i", [P, NB], I32), sb("next_n", [P, NB])
        node_n = sb("node_n", [P, NB])
        src_row = sb("src_row", [P, 2, P], I32)
        x_sb = sb("x_sb", [P, NB, F])
        turned = sb("turned", [P, NP])
        tab_flat = sb("tab_flat", [P, NB * W])
        tab = tab_flat[:, :].rearrange("p (k f) -> p k f", f=W)
        ring_a, ring_b = sb("ring_a", [P, NB * W]), sb("ring_b", [P, NB * W])
        src_i, dst_i = sb("src_i", [P, L], I32), sb("dst_i", [P, L], I32)
        srcT_i = src_i
        neg_wide, ad_wide = sb("neg_wide", [P, BL]), sb("ad_wide", [P, BL])
        neg, ad_exp = neg_wide[:, 0:L], ad_wide[:, 0:L]
        chunk_dst, rank = ad_wide[:, :].bitcast(I32), neg_wide
        pair = sb("pair", [P, 2, BL], BF16)
        fresh = ring_b[:, 0:BL]
        before = sb("before", [P, 1], I32)
        first_rank, first_rank_i = sb("first_rank", [P, CB]), sb("first_rank_i", [P, CB], I32)
        total, iota_col = sb("total", [P, 2]), sb("iota_col", [P, 1])
        first_row = sb("first_row", [1, P * CB], I32)
        onto, scanned = sb("onto", [P, 3, 512]), sb("scanned", [P, 2, 512])
        weights = {n: sb(n, [P, w]) for n, w in (
            ("W1", F), ("W2a", F), ("W2b", F), ("Wpq", 2 * F), ("W3", F), ("Wt", F))}
        conv_w = [sb(f"conv_w{c}", [P, W]) for c in range(2)]
        b1_col = sb("b1_col", [P, 1])
        att_cols = [sb(f"att{c}", [P, 2]) for c in range(2)]
        bias = {n: sb(n + "_rows", [P, F]) for n in ("b2", "b3", "c1", "c2")}
        NC13 = -(-CHUNKS // P)
        cf_i, cf_part = sb("cf_i", [P, NC13], I32), sb("cf_part", [P, 2, NC13], I32)
        cf_f = sb("cf_f", [P, 2, NC13])
        onehot = sb("onehot", [P, 2, P])
        small = {n: sb(n, [P, NB]) for n in (
            "cnt", "base", "cfle", "row_f", "ends", "starts", "empty", "negE", "s0", "s1", "s3",
            "rstd", "ad", "rmax")}
        row_i, end_i, start_i, place_i = (sb(n, [P, NB], I32) for n in ("row_i", "end_i", "start_i", "place_i"))
        zero_wide = sb("zero_wide", [P, L // 3])
        zero_tile = zero_wide[:, 0:W]
        assert L % 3 == 0
        rows = {n: sb("r_" + n, [P, P]) for n in ("dfirst", "dlast", "link", "adl", "rs", "ma", "ms", "l", "cc")}
        state, state_shift = sb("state", [P, P]), sb("state_shift", [P, 3, P])
        fix, fix_s, fix_i = sb("fix", [P, W]), sb("fix_s", [P, 5]), sb("fix_i", [P, 1], I32)
        first_start_i, first_bounds = sb("first_start_i", [P, 1], I32), sb("first_bounds", [P, 2])
        bounds_sb, fix_f = sb("bounds_sb", [P, NB, 2]), sb("fix_f", [P, 3])
        stats, moments = sb("stats", [P, NB, 6]), sb("moments", [P, NB, 2])
        dcol = sb("dcol", [P, 2])
        m1T = sb("m1T", [P, 2, 512])
        gz, gm, gd, gw = (sb(n, [P, G]) for n in ("gz", "gt", "gd", "gw"))
        gmm = sb("gmm", [P, 2, G1 + 1])
        ge, gc = sb("ge", [P, 2, G]), sb("gc", [P, 2, G])
        ad_first = sb("ad_first", [P, 1])
        ps = [ctx.enter_context(nc.psum_tensor(f"ps{i}", [P, 512], F32)) for i in range(8)]

        vec, act, pe, gp = signal("vec"), signal("act"), signal("pe"), signal("gp")
        loads = {n: signal("ld_" + n) for n in ("x", "w", "edges", "cf", "chunks", "firsts", "srcT", "fix", "rows", "ad", "adx")}
        stores = {n: signal("st_" + n) for n in ("tabs", "compact0", "pscatter", "ranks", "h", "bounds", "fix", "zero", "adscatter", "out")}
        q_sem = [signal(f"q_slot{i}") for i in range(RING)]
        w_sem = [signal(f"w_slot{i}") for i in range(WR)]
        b_sem = [signal(f"b_slot{i}") for i in range(WR)]
        node_sem = [signal(f"nodes{i}") for i in range(len(batches))]
        ends_got = {}
        row_sem = [signal(f"src_row{i}") for i in range(2)]
        s_sem = [signal(f"s_slot{i}") for i in range(RING)]

        flat = t["dst"].rearrange("p l -> (p l)")
        flat_dst = flat.rearrange("(c e) -> c e", e=P)
        padded = gp.after(pool.memset(cf_i[:, :], NP + P))
        wait(sync, padded)
        with nc.allow_non_contiguous_dma(reason="one value of every 128, once"):
            whole = CHUNKS // P
            loads["cf"].after(sync.dma_start(cf_i[:, 0:whole], flat_dst[0:whole * P, 0:1].rearrange("(k p) a -> p (k a)", p=P)), 16)
            cf_ready = loads["cf"].after(sync.dma_start(cf_i[0:CHUNKS - whole * P, whole:whole + 1], flat_dst[whole * P:CHUNKS, 0:1]), 16)
        for m, value in ((ident, 0.0), (ones, 1.0), (tri, 1.0), (shift, 0.0), (wrap, 0.0), (zero_wide, 0.0)):
            made = gp.after(pool.memset(m[:, :], value))
        wait(pool, made)
        for m, op, fill, base, step, cm in ((ident, ALU.not_equal, 1.0, 0, -1, 1), (tri, ALU.is_ge, 0.0, 0, 1, -1),
                                            (shift, ALU.not_equal, 1.0, 1, -1, 1), (wrap, ALU.not_equal, 1.0, 1 - P, -1, 1)):
            gp.after(pool.affine_select(out=m[:, :], in_=m[:, :], compare_op=op, fill=fill, base=base,
                                        pattern=[[step, P]], channel_multiplier=cm))
        gp.after(pool.iota(iota_i[:, :], pattern=[[1, P]], base=0, channel_multiplier=0))
        gp.after(pool.iota(iota_col_i[:, :], pattern=[[0, 1]], base=0, channel_multiplier=1))
        consts = gp.after(pool.iota(next_i[:, :], pattern=[[P, NB]], base=1, channel_multiplier=1))
        gp.after(pool.memset(x_sb[:, NB - 1, :], 0.0))
        gp.after(pool.memset(chunk_dst, N))
        blank = gp.after(pool.memset(before[:, :], -1))

        wait(sync, blank)
        x_in = t["x"][0:FULL * P, :].rearrange("(k p) f -> p k f", p=P)
        loads["x"].after(sync.dma_start(x_sb[:, 0:FULL, :], x_in), 16)
        x_ready = loads["x"].after(sync.dma_start(x_sb[0:REST, FULL, :], t["x"][FULL * P:N, :]), 16)
        full, rest = P * L // BL, P * L % BL
        loads["chunks"].after(sync.dma_start(chunk_dst[0:full, :], flat[0:full * BL].rearrange("(p l) -> p l", l=BL)), 16)
        loads["chunks"].after(sync.dma_start(chunk_dst[full:full + 1, 0:rest], flat[full * BL:].rearrange("(a l) -> a l", a=1)), 16)
        with nc.allow_non_contiguous_dma(reason="one value for each partition, once"):
            chunks_ready = loads["chunks"].after(sync.dma_start(
                before[1:full + 1, :], flat[0:full * BL].rearrange("(p l) -> p l", l=BL)[:, BL - 1:BL]), 16)
        srcT_ready = loads["srcT"].after(sync.dma_start(srcT_i[:, :], t["srcT"]), 16)
        edges_ready = loads["edges"].after(sync.dma_start(dst_i[:, :], t["dst"]), 16)
        ld = loads["w"]
        W2 = t["W2"]

        def column(name):
            return t[name].rearrange("(p a) -> p a", a=1)

        for dst, srcap in (
            (weights["W1"][:, :], t["W1"]), (b1_col[:, :], column("b1")),
            (weights["W2a"][:, :], W2[0:F, :]), (weights["W2b"][:, :], W2[F:2 * F, :]),
            (bias["b2"][:, :], t["b2"].rearrange("(a f) -> a f", a=1).broadcast_to([P, F])),
            (weights["W3"][:, :], t["W3"]), (conv_w[0][:, 0:F], t["C1"]), (conv_w[1][:, 0:F], t["C2"]),
            (att_cols[0][:, 0:1], column("as1")), (att_cols[0][:, 1:2], column("ad1")),
            (att_cols[1][:, 0:1], column("as2")), (att_cols[1][:, 1:2], column("ad2")),
        ) + tuple((bias[n][:, :], t[k].rearrange("(a f) -> a f", a=1).broadcast_to([P, F]))
                  for n, k in (("b3", "b3"), ("c1", "cb1"), ("c2", "cb2"))):
            w_ready = ld.after(scalar.dma_start(dst, srcap), 16)
        wait(scalar, made)
        compact_zeroed = stores["compact0"].after(scalar.dma_start(
            P_compact.rearrange("(k p) f -> p k f", p=P), zero_tile[:, 0:F].unsqueeze(1).to_broadcast([P, WINDOWS // P, F])), 16)

        zero_stored = stores["zero"].after(scalar.dma_start(
            ad_edges.rearrange("(p c l) a -> p c (l a)", p=P, c=3), zero_wide[:, 0:L // 3].unsqueeze(1).to_broadcast([P, 3, L // 3])), 16)
        wait(vector, consts, cf_ready)
        vec.after(vector.tensor_copy(iota_row[:, :], iota_i[:, :]))
        vec.after(vector.tensor_copy(next_n[:, :], next_i[:, :]))
        vec.after(vector.tensor_scalar(node_n[:, :], next_i[:, :], -1.0, None, ALU.add))
        vec.after(vector.tensor_copy(iota_col[:, :], iota_col_i[:, :]))
        vec.after(vector.tensor_scalar(cf_part[:, 0, :], cf_i[:, :], P - 1, None, ALU.bitwise_and))
        m = vec.after(vector.tensor_scalar(cf_part[:, 1, :], cf_i[:, :], 7, None, ALU.logical_shift_right))
        wait(vector, m)
        m = vec.after(vector.tensor_copy(cf_f[:, :, :], cf_part[:, :, :]))

        used = None
        for k in range(NC13):
            wait(vector, m, *([used] if used else []))
            vec.after(vector.tensor_scalar(onehot[:, 0, :], iota_row[:, :], cf_f[:, 0, k:k + 1], None, ALU.is_equal))
            hot = vec.after(vector.tensor_scalar(onehot[:, 1, 0:NB], iota_row[:, 0:NB], cf_f[:, 1, k:k + 1], None, ALU.is_equal))
            wait(tensor, hot)
            used = pe.after(tensor.matmul(ps[0][:, 0:NB], lhsT=onehot[:, 0, :], rhs=onehot[:, 1, 0:NB],
                                          start=(k == 0), stop=(k == NC13 - 1)))
        wait(vector, used)
        m = vec.after(vector.tensor_copy(small["cnt"][:, :], ps[0][:, 0:NB]))

        def count_up(o, values, ready):
            wait(tensor, ready)
            pe.after(tensor.matmul(ps[1][:, 0:NB], lhsT=tri[:, :], rhs=values, start=True, stop=True))
            m = pe.after(tensor.matmul(ps[2][:, 0:NB], lhsT=ones[:, :], rhs=values, start=True, stop=True))
            wait(vector, m)
            m = vec.after(vector.tensor_copy(small["s0"][:, :], ps[2][:, 0:NB]))
            wait(vector, m)
            m = vec.after(vector.tensor_tensor_scan(small["base"][:, :], ones[:, 0:NB], small["s0"][:, :], 0.0, ALU.mult, ALU.add))
            wait(vector, m)
            m = vec.after(vector.tensor_tensor(small["base"][:, :], small["base"][:, :], small["s0"][:, :], ALU.subtract))
            wait(vector, m)
            return vec.after(vector.tensor_tensor(o, ps[1][:, 0:NB], small["base"][:, :], ALU.add))

        m = count_up(small["cfle"][:, :], small["cnt"][:, :], m)
        wait(vector, m)
        m = vec.after(vector.tensor_scalar(small["row_f"][:, :], small["cfle"][:, :], -1.0, 0.0, ALU.add, ALU.max))
        wait(vector, m)
        m = vec.after(vector.tensor_copy(row_i[:, :], small["row_f"][:, :]))
        wait(pool, m)
        dst_rows = ring_a[:, :].bitcast(I32)[:, 0:NP].rearrange("p (k e) -> p k e", e=P)
        for k in range(NB):
            rows_gathered = loads["rows"].after(pool.indirect_dma_start(
                out=dst_rows[:, k, :], out_offset=None, in_=flat_dst,
                in_offset=bass.IndirectOffsetOnAxis(ap=row_i[:, k:k + 1], axis=0)), 16)
        wait(vector, chunks_ready)
        vec.after(vector.tensor_tensor(fresh[:, 1:BL], chunk_dst[:, 1:BL], chunk_dst[:, 0:BL - 1], ALU.not_equal))
        m2 = vec.after(vector.tensor_tensor(fresh[:, 0:1], chunk_dst[:, 0:1], before[:, :], ALU.not_equal))
        wait(vector, m2)
        vec.after(vector.tensor_scalar(pair[:, 1, :], fresh[:, :], -BIG, None, ALU.mult))
        m2 = vec.after(vector.tensor_tensor_scan(rank[:, :], ones[:, 0:1].to_broadcast([P, BL]), fresh[:, :], 0.0, ALU.mult, ALU.add))
        wait(vector, m2)
        m2 = vec.after(vector.tensor_copy(total[:, 0:1], rank[:, BL - 1:BL]))
        wait(tensor, m2)
        m2 = pe.after(tensor.matmul(ps[3][:, 0:1], lhsT=tri[:, :], rhs=total[:, 0:1], start=True, stop=True))
        wait(vector, m2)
        m2 = vec.after(vector.tensor_tensor(total[:, 1:2], ps[3][:, 0:1], total[:, 0:1], ALU.subtract))
        wait(vector, m2)
        firsts = rank[:, :].rearrange("p (c e) -> p c e", e=P)[:, :, 0]
        m2 = vec.after(vector.tensor_copy(first_rank[:, :], firsts))
        wait(vector, m2)
        vec.after(vector.tensor_tensor(pair[:, 0, :].rearrange("p (c e) -> p c e", e=P), rank[:, :].rearrange("p (c e) -> p c e", e=P),
                                       first_rank[:, :].unsqueeze(2).to_broadcast([P, CB, P]), ALU.subtract))
        m2 = vec.after(vector.tensor_scalar(first_rank_i[:, :], first_rank[:, :], total[:, 1:2], -1.0, ALU.add, ALU.add))
        wait(sync, m2)
        stores["ranks"].after(sync.dma_start(rank_rows.rearrange("s (p l) -> p s l", p=P), pair[:, :, :]), 16)
        ranks_stored = stores["ranks"].after(sync.dma_start(first_ranks.rearrange("a (p c) -> p (a c)", p=P), first_rank_i[:, :]), 16)
        wait(sync, ranks_stored)
        firsts_ready = loads["firsts"].after(sync.dma_start(first_row[:, :], first_ranks), 16)

        def turn(source, ready):
            wait(tensor, ready)
            free = {}
            for q, k0 in enumerate(range(0, NB, 4)):
                bank, ks = ps[6 + q % 2], range(k0, min(k0 + 4, NB))
                if q % 2 in free:
                    wait(tensor, free[q % 2])
                for k in ks:
                    mark = pe.after(tensor.transpose(bank[:, (k - k0) * P:(k - k0 + 1) * P], source[:, k, 0:F], ident[:, :]))
                wait(scalar, mark)
                n = len(ks) * P
                free[q % 2] = act.after(scalar.activation(turned[:, k0 * P:k0 * P + n], bank[:, 0:n], ACT.Copy))
            return free[q % 2]

        wait(vector, w_ready)
        vec.after(vector.tensor_tensor(weights["Wpq"][:, 0:F], weights["W2a"][:, :], weights["W2b"][:, :], ALU.subtract))
        folded = vec.after(vector.tensor_copy(weights["Wpq"][:, F:2 * F], weights["W2b"][:, :]))

        turned_x = turn(x_sb, x_ready)
        wait(tensor, w_ready, turned_x, folded)
        free = {}
        for q, c0 in enumerate(range(0, NP, 512)):
            n = min(512, NP - c0)
            b = 2 + q % 2
            if b in free:
                wait(tensor, free[b])
            mark = pe.after(tensor.matmul(ps[b][:, 0:n], lhsT=weights["W1"][:, :], rhs=turned[:, c0:c0 + n], start=True, stop=True))
            wait(scalar, mark)
            free[b] = act.after(scalar.activation(turned[:, c0:c0 + n], ps[b][:, 0:n], ACT.Identity, bias=b1_col[:, 0:1]))
        h_ready = free[b]
        wait(tensor, h_ready, folded)
        p_stage, q_stage = nodes(tab_flat, F), nodes(ring_b, F)
        free = {}
        for q, k0 in enumerate(range(0, NB, 2)):
            ks = range(k0, min(k0 + 2, NB))
            b = 4 + q % 2
            if b in free:
                wait(tensor, free[b])
            for i, k in enumerate(ks):
                mark = pe.after(tensor.matmul(ps[b][:, i * 256:(i + 1) * 256], lhsT=turned[:, k * P:(k + 1) * P],
                                              rhs=weights["Wpq"][:, :], start=True, stop=True))
            wait(vector, mark)
            n = len(ks)
            both = ps[b][:, 0:n * 256].rearrange("p (k s f) -> p k s f", s=2, f=F)
            p_free = vec.after(vector.tensor_tensor(p_stage[:, k0:k0 + n, :], both[:, :, 0, :],
                                                    bias["b2"][:, :].unsqueeze(1).to_broadcast([P, n, F]), ALU.add))
            wait(scalar, p_free)
            free[b] = act.after(scalar.activation(q_stage[:, k0:k0 + n, :], both[:, :, 1, :], ACT.Copy))
        pq_ready, p_ready = free[b], p_free
        wait(sync, pq_ready)
        tables_stored = stores["tabs"].after(sync.dma_start(Q_table.rearrange("(k p) f -> p k f", p=P), q_stage), 16)

        wait(vector, rows_gathered)
        below = ring_a[:, 0:NP].rearrange("p (k e) -> p k e", e=P)
        m = vec.after(vector.tensor_tensor(below, dst_rows, next_n[:, :].unsqueeze(2).to_broadcast([P, NB, P]), ALU.is_lt))
        wait(vector, m)
        m = vec.after(vector.tensor_reduce(small["s0"][:, :], below, AX_X, ALU.add))
        wait(vector, m)
        m = ends_ready = vec.after(vector.scalar_tensor_tensor(out=small["ends"][:, :], in0=small["row_f"][:, :], scalar=float(P),
                                                  in1=small["s0"][:, :], op0=ALU.mult, op1=ALU.add))
        rows_free = m
        wait(tensor, m)
        tensor.matmul(ps[1][:, 0:NB], lhsT=shift[:, :], rhs=small["ends"][:, :], start=True, stop=False)
        m = pe.after(tensor.matmul(ps[1][:, 1:NB], lhsT=wrap[:, :], rhs=small["ends"][:, 0:NB - 1], start=False, stop=True))
        wait(vector, m)
        m = vec.after(vector.tensor_copy(small["starts"][:, :], ps[1][:, 0:NB]))
        wait(vector, m)
        s = small

        def chain(instructions):
            mark = None
            for make in instructions:
                mark = vec.after(make())
                wait(vector, mark)
            return mark

        index_ready = chain([
            lambda: vector.tensor_tensor(s["empty"][:, :], s["ends"][:, :], s["starts"][:, :], ALU.is_equal),
            lambda: vector.tensor_scalar(s["negE"][:, :], s["empty"][:, :], -BIG, None, ALU.mult),
            lambda: vector.scalar_tensor_tensor(out=s["s0"][:, :], in0=s["empty"][:, :], scalar=1.0e6, in1=s["starts"][:, :],
                                                op0=ALU.mult, op1=ALU.add),
            lambda: vector.tensor_copy(start_i[:, :], s["s0"][:, :]),
            lambda: vector.tensor_scalar(s["s0"][:, :], s["ends"][:, :], -1.0, 0.0, ALU.add, ALU.max),
            lambda: vector.tensor_copy(end_i[:, :], s["s0"][:, :]),
            lambda: vector.tensor_scalar(s["cnt"][:, :], s["empty"][:, :], -1.0, 1.0, ALU.mult, ALU.add),
        ])
        m = count_up(s["s3"][:, :], s["cnt"][:, :], index_ready)
        wait(vector, m)
        rank_index = chain([
            lambda: vector.scalar_tensor_tensor(out=s["s3"][:, :], in0=s["empty"][:, :], scalar=1.0e6, in1=s["s3"][:, :],
                                                op0=ALU.mult, op1=ALU.add),
            lambda: vector.tensor_scalar(s["s3"][:, :], s["s3"][:, :], -1.0, None, ALU.add),
            lambda: vector.tensor_copy(place_i[:, :], s["s3"][:, :]),
        ])
        wait(vector, ranks_stored)
        m2 = vec.after(vector.tensor_tensor(neg[:, 1:L], dst_i[:, 1:L], dst_i[:, 0:L - 1], ALU.not_equal))
        vec.after(vector.memset(neg[:, 0:1], -BIG))
        wait(vector, m2)
        neg_ready = vec.after(vector.tensor_scalar(neg[:, 1:L], neg[:, 1:L], -BIG, None, ALU.mult))
        vec.after(vector.tensor_copy(dcol[:, 0:1], dst_i[:, 0:1]))
        dcol_ready = vec.after(vector.tensor_copy(dcol[:, 1:2], dst_i[:, L - 1:L]))


        def spread(column, bank):
            return pe.after(tensor.matmul(bank, lhsT=column.to_broadcast([P, P]), rhs=ident[:, :], start=True, stop=True))

        vec.after(vector.tensor_copy(bounds_sb[:, :, 0], s["starts"][:, :]))
        m = vec.after(vector.tensor_copy(bounds_sb[:, :, 1], s["ends"][:, :]))
        wait(sync, m)
        bounds_stored = stores["bounds"].after(sync.dma_start(bounds_table.rearrange("(k p) a -> p k a", p=P), bounds_sb[:, :, :]), 16)
        wait(tensor, dcol_ready, rank_index)
        spread(dcol[:, 0:1], ps[0][:, 0:P])
        m = spread(dcol[:, 1:2], ps[1][:, 0:P])
        wait(vector, m)
        r = rows
        vec.after(vector.tensor_copy(r["dfirst"][:, :], ps[0][:, 0:P]))
        chain([
            lambda: vector.tensor_copy(r["dlast"][:, :], ps[1][:, 0:P]),
            lambda: vector.memset(r["link"][:, :], 0.0),
            lambda: vector.tensor_tensor(r["link"][:, 1:P], r["dfirst"][:, 1:P], r["dlast"][:, 0:P - 1], ALU.is_equal),
            lambda: vector.tensor_tensor(r["cc"][:, :], r["dfirst"][:, :], r["dlast"][:, :], ALU.is_equal),
            lambda: vector.tensor_tensor(r["link"][:, :], r["link"][:, :], r["cc"][:, :], ALU.mult),
        ])
        link_ready = chain([lambda: vector.tensor_scalar(r["link"][:, :], r["link"][:, :], -1.0, BIG, ALU.add, ALU.mult)])

        wait(pool, p_ready, rank_index, compact_zeroed)
        for k in range(NB):
            p_scattered = stores["pscatter"].after(pool.indirect_dma_start(
                out=P_compact, out_offset=bass.IndirectOffsetOnAxis(ap=place_i[:, k:k + 1], axis=0),
                in_=p_stage[:, k, :], in_offset=None, bounds_check=WINDOWS - 1, oob_is_err=False), 16)

        wait(pool, bounds_stored, edges_ready)
        bounds_got = loads["fix"].after(pool.indirect_dma_start(
            out=first_bounds[:, :], out_offset=None, in_=bounds_table,
            in_offset=bass.IndirectOffsetOnAxis(ap=dst_i[:, 0:1], axis=0)), 16)

        q_ring = ring_a[:, 0:RING * G * F].rearrange("p (s g f) -> p s g f", s=RING, f=F)
        w_ring = turned[:, 0:WR * G * F].rearrange("p (s g f) -> p s g f", s=WR, f=F)
        b_ring = tab_flat[:, :].bitcast(BF16)[:, 0:WR * 2 * G * P].rearrange("p (s r e) -> p s r e", s=WR, r=2)
        o_ring = ring_b[:, 0:RING * G * F].rearrange("p (s g f) -> p s g f", s=RING, f=F)
        wait(pool, tables_stored)
        wait(sync, p_scattered, firsts_ready, pq_ready)
        wait(scalar, tables_stored)
        quads = [(g, a, min(4, j1 - j0 - a)) for g, (j0, j1) in enumerate(groups) for a in range(0, j1 - j0, 4)]
        last_of = {g: i for i, (g, a, n) in enumerate(quads)}
        placed, relued, multiplied, scan_done, turned_back, evacuated, stored = {}, {}, {}, {}, {}, {}, {}
        gathered, windowed, hot = {}, {}, {}

        def gather_q(g):
            j0, j1 = groups[g]
            slot = g % RING
            if g >= RING:
                wait(pool, placed[last_of[g - RING]])
            for j in range(j0, j1):
                gathered[g] = q_sem[slot].after(pool.indirect_dma_start(
                    out=q_ring[:, slot, j - j0, :], out_offset=None, in_=Q_table,
                    in_offset=bass.IndirectOffsetOnAxis(ap=srcT_i[:, j:j + 1], axis=0)), 16)

        def load_windows(g):
            j0, j1 = groups[g]
            slot = g % WR
            if g >= WR:
                wait(sync, placed[last_of[g - WR]], scan_done[last_of[g - WR]])
            b = b_sem[slot].after(sync.dma_start(
                b_ring[:, slot, :, 0:(j1 - j0) * P],
                rank_rows[:, j0 * P:j1 * P].unsqueeze(0).to_broadcast([P, 2, (j1 - j0) * P])), 16)
            for j in range(j0, j1, 4):
                n = min(4, j1 - j)
                _, at = nc.values_load_multi_w_load_instructions(first_row[0:1, j:j + n], engines=[sync.engine],
                                                                 min_val=0, max_val=WINDOWS - P)
                for i in range(n):
                    w = w_sem[slot].after(sync.dma_start(w_ring[:, slot, j + i - j0, :], P_compact[bass.ds(at[i], P), :]), 16)
            windowed[g] = (w, b)

        def spread_ranks(i):
            g, a, n = quads[i]
            if i >= 3:
                wait(vector, placed[i - 3])
            wait(vector, windowed[g][1])
            hot[i] = vec.after(vector.tensor_scalar(onto[:, i % 3, 0:n * P], b_ring[:, g % WR, 0, a * P:(a + n) * P],
                                                    iota_col[:, 0:1], None, ALU.is_equal))

        def stage_a(i):
            g, a, n = quads[i]
            b = i % 2
            if i >= 2:
                wait(tensor, relued[i - 2])
            wait(tensor, gathered[g], windowed[g][0], hot[i])
            for c in range(n):
                piece = ps[b][:, c * P:(c + 1) * P]
                pe.after(tensor.matmul(piece, lhsT=q_ring[:, g % RING, a + c, :], rhs=ident[:, :], start=True, stop=False))
                placed[i] = pe.after(tensor.matmul(piece, lhsT=w_ring[:, g % WR, a + c, :], rhs=onto[:, i % 3, c * P:(c + 1) * P],
                                                   start=False, stop=True))
            if i >= 2:
                wait(scalar, multiplied[i - 2])
            wait(scalar, placed[i])
            relued[i] = act.after(scalar.activation(m1T[:, b, 0:n * P], ps[b][:, 0:n * P], ACT.Relu))

        def stage_b(i):
            g, a, n = quads[i]
            b = i % 2
            if i >= 2:
                wait(tensor, scan_done[i - 2])
            wait(tensor, relued[i])
            multiplied[i] = pe.after(tensor.matmul(ps[2 + b][:, 0:n * P], lhsT=weights["W3"][:, :], rhs=m1T[:, b, 0:n * P],
                                                   start=True, stop=True))
            if i >= 2:
                wait(vector, turned_back[i - 2])
            if i >= 1:
                wait(vector, scan_done[i - 1])
            wait(vector, multiplied[i])
            initial = scanned[:, 1 - b, quads[i - 1][2] * P - 1:quads[i - 1][2] * P] if i else 0.0
            scan_done[i] = vec.after(vector.tensor_tensor_scan(
                scanned[:, b, 0:n * P], b_ring[:, g % WR, 1, a * P:(a + n) * P], ps[2 + b][:, 0:n * P], initial, ALU.add, ALU.max))

        def stage_c(i):
            g, a, n = quads[i]
            b, slot = i % 2, g % RING
            if i >= 2:
                wait(tensor, evacuated[i - 2])
            wait(tensor, scan_done[i])
            for c in range(n):
                turned_back[i] = pe.after(tensor.transpose(ps[4 + b][:, c * P:(c + 1) * P], scanned[:, b, c * P:(c + 1) * P], ident[:, :]))
            if a == 0 and g >= RING:
                wait(scalar, stored[g - RING])
            wait(scalar, turned_back[i])
            evacuated[i] = act.after(scalar.activation(o_ring[:, slot, a:a + n, :],
                                                       ps[4 + b][:, 0:n * P].rearrange("p (c f) -> p c f", f=F), ACT.Copy))
            if i == last_of[g]:
                j0, j1 = groups[g]
                wait(sync, evacuated[i])
                stored[g] = s_sem[slot].after(sync.dma_start(
                    run_max.rearrange("(c p) f -> p c f", p=P)[:, j0:j1, :], o_ring[:, slot, 0:j1 - j0, :]), 16)

        wait(pool, srcT_ready)
        load_windows(0)
        load_windows(1)
        wait(vector, bounds_got)
        b0, b1 = first_bounds[:, 0:1], first_bounds[:, 1:2]
        chain([
            lambda: vector.tensor_copy(first_start_i[:, :], b0),
            lambda: vector.tensor_scalar(fix_f[:, 2:3], iota_col[:, :], float(L), None, ALU.mult),
            lambda: vector.tensor_tensor(fix_f[:, 0:1], b0, fix_f[:, 2:3], ALU.is_ge),
            lambda: vector.tensor_scalar(fix_f[:, 1:2], b1, float(L), None, ALU.subtract),
            lambda: vector.tensor_tensor(fix_f[:, 1:2], fix_f[:, 1:2], fix_f[:, 2:3], ALU.is_gt),
            lambda: vector.tensor_tensor(fix_f[:, 0:1], fix_f[:, 0:1], fix_f[:, 1:2], ALU.max),
            lambda: vector.scalar_tensor_tensor(out=fix_f[:, 0:1], in0=fix_f[:, 0:1], scalar=1.0e6, in1=b1, op0=ALU.mult, op1=ALU.add),
            lambda: vector.tensor_scalar(fix_f[:, 0:1], fix_f[:, 0:1], -1.0, None, ALU.add),
            lambda: vector.tensor_copy(fix_i[:, :], fix_f[:, 0:1]),
        ])
        w_made = {}
        for layer in range(2):
            w = conv_w[layer]
            wait(tensor, w_ready)
            m = pe.after(tensor.transpose(ps[6][:, 0:P], w[:, 0:F], ident[:, :]))
            wait(vector, m)
            m = vec.after(vector.tensor_copy(weights["Wt"][:, :], ps[6][:, 0:P]))
            wait(tensor, m)
            m = pe.after(tensor.matmul(ps[7][:, 0:2], lhsT=weights["Wt"][:, :], rhs=att_cols[layer][:, :], start=True, stop=True))
            wait(vector, m)
            w_made[layer] = vec.after(vector.tensor_copy(w[:, F:W], ps[7][:, 0:2]))
        spread_ranks(0)
        for i in range(len(quads) + 2):
            if i < len(quads):
                g, a, n = quads[i]
                if a == 0:
                    gather_q(g)
                stage_a(i)
            if i + 1 < len(quads):
                spread_ranks(i + 1)
            if 0 <= i - 1 < len(quads):
                stage_b(i - 1)
            if i < len(quads) and a == 0 and g + 2 < len(groups):
                load_windows(g + 2)
            if i >= 2:
                stage_c(i - 2)
        last_quad = len(quads) - 1

        def over(small_ap, width):
            return small_ap.unsqueeze(2).to_broadcast([P, small_ap.shape[1], width])

        def gather_ends(table, view):
            for b, (k0, k1) in enumerate(batches):
                for k in range(k0, k1):
                    ends_got[b] = node_sem[b].after(pool.indirect_dma_start(
                        out=view[:, k, :], out_offset=None, in_=table,
                        in_offset=bass.IndirectOffsetOnAxis(ap=end_i[:, k:k + 1], axis=0)), 16)

        def layernorm(y, k0, k1):
            for k in range(k0, k1):
                m = vec.after(vector.bn_stats(stats[:, k, :], y[:, k, :]))
            wait(vector, m)
            for k in range(k0, k1):
                m = vec.after(vector.bn_aggr(moments[:, k, :], stats[:, k, :]))
            wait(vector, m)
            m = vec.after(vector.tensor_scalar(s["rstd"][:, k0:k1], moments[:, k0:k1, 1], EPS, None, ALU.add))
            wait(scalar, m)
            m = act.after(scalar.activation(s["rstd"][:, k0:k1], s["rstd"][:, k0:k1], ACT.Sqrt))
            wait(vector, m)
            m = vec.after(vector.reciprocal(s["rstd"][:, k0:k1], s["rstd"][:, k0:k1]))
            wait(vector, m)
            for k in range(k0, k1):
                m = vec.after(vector.tensor_scalar(y[:, k, :], y[:, k, :], moments[:, k, 0:1], s["rstd"][:, k:k + 1],
                                                   ALU.subtract, ALU.mult))
            return m

        evac_free = {}

        def project(layer, source, function, k0, k1, ready):
            w = conv_w[layer]
            wait(tensor, ready)
            for q, c0 in enumerate(range(k0, k1, 4)):
                bank, n = 6 + q % 2, min(4, k1 - c0)
                if bank in evac_free:
                    wait(tensor, evac_free[bank])
                for k in range(c0, c0 + n):
                    mark = pe.after(tensor.transpose(ps[bank][:, (k - c0) * P:(k - c0 + 1) * P], source[:, k, 0:F], ident[:, :]))
                wait(scalar, mark)
                evac_free[bank] = act.after(scalar.activation(turned[:, c0 * P:(c0 + n) * P], ps[bank][:, 0:n * P], function))
            wait(tensor, evac_free[bank], w_made[layer])
            for q, c0 in enumerate(range(k0, k1, 3)):
                bank, n = 2 + q % 2, min(3, k1 - c0)
                if bank in evac_free:
                    wait(tensor, evac_free[bank])
                for i in range(n):
                    mark = pe.after(tensor.matmul(ps[bank][:, i * W:(i + 1) * W], lhsT=turned[:, (c0 + i) * P:(c0 + i + 1) * P],
                                                  rhs=w[:, :], start=True, stop=True))
                wait(vector, mark)
                blk = ps[bank][:, 0:n * W].rearrange("p (k f) -> p k f", f=W)
                vec.after(vector.tensor_copy(tab[:, c0:c0 + n, F + 1], blk[:, :, F]))
                mark = vec.after(vector.tensor_copy(s["ad"][:, c0:c0 + n], blk[:, :, F + 1]))
                wait(scalar, mark)
                evac_free[bank] = act.after(scalar.activation(tab[:, c0:c0 + n, 0:F], blk[:, :, 0:F], ACT.Copy))
            wait(sync, evac_free[bank])
            h_stored = stores["h"].after(sync.dma_start(
                H_table.rearrange("(k p) f -> p k f", p=P)[:, k0:k1, :], tab[:, k0:k1, :]), 16)
            wait(pool, mark, zero_stored)
            for k in range(k0, k1):
                scattered = stores["adscatter"].after(pool.indirect_dma_start(
                    out=ad_edges, out_offset=bass.IndirectOffsetOnAxis(ap=start_i[:, k:k + 1], axis=0),
                    in_=s["ad"][:, k:k + 1], in_offset=None, bounds_check=P * L - 1, oob_is_err=False), 16)
            return h_stored, scattered

        E = nodes(ring_a, F)
        wait(pool, *list(stored.values())[-RING:], placed[last_quad])
        gather_ends(run_max, E)
        wait(vector, scan_done[last_quad])
        ones_col = vec.after(vector.memset(tab[:, :, F:F + 1], 1.0))
        wait(sync, ones_col)
        wait(scalar, scan_done[last_quad])
        for b, (k0, k1) in enumerate(batches):
            wait(vector, ends_got[b])
            for k in range(k0, k1):
                m = vec.after(vector.scalar_tensor_tensor(out=E[:, k, :], in0=E[:, k, :], scalar=s["negE"][:, k:k + 1],
                                                          in1=bias["b3"][:, :], op0=ALU.add, op1=ALU.add))
            wait(vector, m)
            m = vec.after(vector.scalar_tensor_tensor(out=x_sb[:, k0:k1, :], in0=E[:, k0:k1, :], scalar=0.0,
                                                      in1=x_sb[:, k0:k1, :], op0=ALU.max, op1=ALU.add))
            wait(vector, m)
            m = layernorm(x_sb, k0, k1)
            h_stored, scattered = project(0, x_sb, ACT.Copy, k0, k1, m)
        e_read = m

        wait(sync, gathered[len(groups) - 1])
        src_ready = loads["x"].after(sync.dma_start(src_i[:, :], t["src"]), 16)
        wait(pool, src_ready)
        for layer in range(2):
            wait(sync, scattered)
            m = loads["ad"].after(sync.dma_start(ad_exp[:, :], ad_edges.rearrange("(p l) a -> p (l a)", p=P)), 16)
            wait(pool, scattered)
            m2 = loads["adx"].after(pool.indirect_dma_start(out=ad_first[:, :], out_offset=None, in_=ad_edges,
                                    in_offset=bass.IndirectOffsetOnAxis(ap=first_start_i[:, :], axis=0)), 16)
            wait(vector, m, m2)
            keep = ring_b[:, 0:L]
            ad_ready = chain([
                lambda: vector.tensor_scalar(keep, neg[:, :], 0.0, None, ALU.is_ge),
                lambda: vector.tensor_copy(ad_exp[:, 0:1], ad_first[:, :]),
                lambda: vector.tensor_tensor_scan(ring_b[:, L:2 * L], keep, ad_exp[:, :], 0.0, ALU.mult, ALU.add),
                lambda: vector.tensor_copy(ad_exp[:, :], ring_b[:, L:2 * L]),
            ])

            h_ring = ring_a[:, 0:RING1 * G1 * W].rearrange("p (s g f) -> p s g f", s=RING1, f=W)
            r_ring = ring_b[:, 0:RING1 * G1 * W].rearrange("p (s g f) -> p s g f", s=RING1, f=W)
            wait(pool, h_stored, e_read, evac_free[6], evac_free[7])
            h_free, s_stored, w_used = {}, {}, {}
            row_got, picked, picked_row, row_used = {}, {}, {}, {}
            by_product = [g for g, (j0, j1) in enumerate(groups1) if j1 - j0 == G1]
            hot_ring = turned[:, :].rearrange("p (k e) -> p k e", e=P)

            def load_src_row(g):
                if g - 2 in row_used:
                    wait(sync, row_used[g - 2])
                j = groups1[g][1] - 1
                row_got[g] = row_sem[g % 2].after(sync.dma_start(
                    src_row[:, g % 2, :], t["srcL"][j:j + 1, :].to_broadcast([P, P])), 16)

            def pick(g, c):
                k0, k1 = c * PIECE, min((c + 1) * PIECE, NB)
                if c == 0:
                    wait(vector, row_got[g])
                if (g - 1, c) in picked:
                    wait(vector, picked[g - 1, c])
                hot_mark = row_used[g] = vec.after(vector.tensor_tensor(
                    hot_ring[:, k0:k1, :], src_row[:, g % 2, :].unsqueeze(1).to_broadcast([P, k1 - k0, P]),
                    node_n[:, k0:k1].unsqueeze(2).to_broadcast([P, k1 - k0, P]), ALU.is_equal))
                if c == 0 and g - 2 in picked_row:
                    wait(tensor, picked_row[g - 2])
                wait(tensor, hot_mark)
                for k in range(k0, k1):
                    picked[g, c] = pe.after(tensor.matmul(ps[g % 2][:, 0:W], lhsT=hot_ring[:, k, :], rhs=tab[:, k, :],
                                                          start=(k == 0), stop=(k == NB - 1)))

            def put_row(g):
                slot = g % RING1
                if slot in h_free:
                    wait(scalar, h_free[slot])
                wait(scalar, picked[g, LAST_PIECE])
                picked_row[g] = act.after(scalar.activation(h_ring[:, slot, G1 - 1, :], ps[g % 2][:, 0:W], ACT.Copy))

            LAST_PIECE = (NB - 1) // PIECE
            wait(vector, evac_free[6], evac_free[7], evac_free[2], evac_free[3])
            wait(tensor, ones_col, evac_free[2], evac_free[3])
            wait(scalar, e_read)
            load_src_row(0)
            load_src_row(1)
            for g in range(2):
                for c in range(LAST_PIECE + 1):
                    pick(g, c)
                put_row(g)
            load_src_row(2)
            previous, prev_max = zero_tile[:, 0:F + 1], zero_tile[:, F + 1:W]
            m = vec.after(vector.memset(gmm[:, 1, G1:G1 + 1], 0.0))
            wait(vector, m)
            pn = G1
            for g, (j0, j1) in enumerate(groups1):
                slot, n, par = g % RING1, j1 - j0, g % 2
                if slot in h_free:
                    wait(pool, h_free[slot])
                by_dma = j1 - 1 if g in by_product else j1
                for j in range(j0, by_dma):
                    got = q_sem[slot].after(pool.indirect_dma_start(
                        out=h_ring[:, slot, j - j0, :], out_offset=None, in_=H_table,
                        in_offset=bass.IndirectOffsetOnAxis(ap=src_i[:, j:j + 1], axis=0)), 16)
                wait(vector, got)
                if g in by_product:
                    wait(vector, picked_row[g])
                if slot in s_stored:
                    wait(vector, s_stored[slot])
                a_src = h_ring[:, slot, 0:n, F + 1]
                top = r_ring[:, slot, 0:n, F + 1]
                ngs, ads = neg[:, j0:j1], ad_exp[:, j0:j1]
                mm = gmm[:, par, :]
                m = vec.after(vector.tensor_tensor_scan(top, ngs, a_src, prev_max, ALU.add, ALU.max))
                m2 = vec.after(vector.tensor_tensor(gz[:, 0:n], a_src, ads, ALU.add))
                wait(vector, m)
                m3 = vec.after(vector.tensor_tensor(gd[:, 0:n], top, ads, ALU.add))
                vec.after(vector.tensor_copy(mm[:, 0:1], gmm[:, 1 - par, pn:pn + 1]))
                wait(vector, m3)
                vec.after(vector.scalar_tensor_tensor(out=mm[:, 1:n + 1], in0=gd[:, 0:n], scalar=SLOPE, in1=gd[:, 0:n],
                                                      op0=ALU.mult, op1=ALU.max))
                m2 = vec.after(vector.scalar_tensor_tensor(out=gw[:, 0:n], in0=gz[:, 0:n], scalar=SLOPE, in1=gz[:, 0:n],
                                                           op0=ALU.mult, op1=ALU.max))
                wait(vector, m2)
                if par in w_used:
                    wait(vector, w_used[par])
                vec.after(vector.tensor_tensor(ge[:, par, 0:n], gw[:, 0:n], mm[:, 1:n + 1], ALU.subtract))
                m = vec.after(vector.tensor_tensor(gz[:, 0:n], mm[:, 0:n], mm[:, 1:n + 1], ALU.subtract))
                wait(vector, m)
                m = vec.after(vector.tensor_tensor(gc[:, par, 0:n], gz[:, 0:n], ngs, ALU.add))
                wait(scalar, m)
                act.after(scalar.activation(ge[:, par, 0:n], ge[:, par, 0:n], ACT.Exp))
                m = act.after(scalar.activation(gc[:, par, 0:n], gc[:, par, 0:n], ACT.Exp))
                wait(scalar, m)
                if g + 2 in by_product:
                    pick(g + 2, 0)
                wait(vector, m)
                for i in range(n):
                    scaled = act.after(scalar.activation(h_ring[:, slot, i, 0:F + 1], h_ring[:, slot, i, 0:F + 1], ACT.Copy,
                                                         scale=ge[:, par, i:i + 1]))
                    wait(vector, scaled)
                    last = vec.after(vector.scalar_tensor_tensor(
                        out=r_ring[:, slot, i, 0:F + 1], in0=previous, scalar=gc[:, par, i:i + 1],
                        in1=h_ring[:, slot, i, 0:F + 1], op0=ALU.mult, op1=ALU.add))
                    previous = r_ring[:, slot, i, 0:F + 1]
                    if g + 2 in by_product and i + 1 <= LAST_PIECE:
                        pick(g + 2, i + 1)
                    wait(vector, last)
                    if g and g + 1 in by_product and i == 5:
                        put_row(g + 1)
                prev_max = r_ring[:, slot, n - 1, F + 1:W]
                whole_last = r_ring[:, slot, n - 1, :]
                pn = n
                w_used[par] = scaled
                h_free[slot] = last
                if g + 3 in by_product:
                    load_src_row(g + 3)
                wait(sync, last)
                s_stored[slot] = s_sem[slot].after(sync.dma_start(
                    run_sum.rearrange("(p l) f -> p l f", p=P)[:, j0:j1, :], r_ring[:, slot, 0:n, :]), 16)

            skipped = vec.after(vector.memset(fix[:, :], 0.0))
            wait(pool, skipped, *s_stored.values())
            fix_got = loads["fix"].after(pool.indirect_dma_start(
                out=fix[:, :], out_offset=None, in_=run_sum, in_offset=bass.IndirectOffsetOnAxis(ap=fix_i[:, :], axis=0),
                bounds_check=P * L - 1, oob_is_err=False), 16)

            wait(tensor, last)
            pe.after(tensor.transpose(ps[4][:, 0:P], whole_last[:, 0:F], ident[:, :]))
            spread(whole_last[:, F + 1:W], ps[5][:, 0:P])
            spread(ad_exp[:, L - 1:L], ps[6][:, 0:P])
            m = spread(whole_last[:, F:F + 1], ps[7][:, 0:P])
            wait(vector, m)
            m = chain([
                lambda: vector.tensor_copy(r["adl"][:, :], ps[6][:, 0:P]),
                lambda: vector.tensor_tensor_scan(r["rs"][:, :], r["link"][:, :], ps[5][:, 0:P], -BIG, ALU.add, ALU.max),
                lambda: vector.tensor_tensor(r["ma"][:, :], ps[5][:, 0:P], r["adl"][:, :], ALU.add),
                lambda: vector.scalar_tensor_tensor(out=r["ma"][:, :], in0=r["ma"][:, :], scalar=SLOPE, in1=r["ma"][:, :], op0=ALU.mult, op1=ALU.max),
                lambda: vector.tensor_tensor(r["ms"][:, :], r["rs"][:, :], r["adl"][:, :], ALU.add),
                lambda: vector.scalar_tensor_tensor(out=r["ms"][:, :], in0=r["ms"][:, :], scalar=SLOPE, in1=r["ms"][:, :], op0=ALU.mult, op1=ALU.max),
                lambda: vector.tensor_tensor(r["ma"][:, :], r["ma"][:, :], r["ms"][:, :], ALU.subtract),
                lambda: vector.memset(r["cc"][:, :], 0.0),
                lambda: vector.tensor_tensor(r["cc"][:, 1:P], r["ms"][:, 0:P - 1], r["ms"][:, 1:P], ALU.subtract),
                lambda: vector.tensor_tensor(r["cc"][:, :], r["cc"][:, :], r["link"][:, :], ALU.add),
            ])
            wait(scalar, m)
            act.after(scalar.activation(r["ma"][:, :], r["ma"][:, :], ACT.Exp))
            m = act.after(scalar.activation(r["cc"][:, :], r["cc"][:, :], ACT.Exp))
            wait(vector, m)
            m = chain([
                lambda: vector.tensor_tensor(r["l"][:, :], ps[7][:, 0:P], r["ma"][:, :], ALU.mult),
                lambda: vector.tensor_tensor(r["ma"][:, :], ps[4][:, 0:P], r["ma"][:, :], ALU.mult),
                lambda: vector.memset(state_shift[:, :, :], 0.0),
                lambda: vector.tensor_tensor_scan(state[:, :], r["cc"][:, :], r["ma"][:, :], 0.0, ALU.mult, ALU.add),
                lambda: vector.tensor_copy(state_shift[:, 0, 1:P], state[:, 0:P - 1]),
                lambda: vector.tensor_tensor_scan(state[:, :], r["cc"][:, :], r["l"][:, :], 0.0, ALU.mult, ALU.add),
                lambda: vector.tensor_copy(state_shift[:, 1, 1:P], state[:, 0:P - 1]),
                lambda: vector.tensor_copy(state_shift[:, 2, 1:P], r["rs"][:, 0:P - 1]),
            ])
            wait(tensor, m)
            for i in range(3):
                m = pe.after(tensor.transpose(ps[4 + i][:, 0:P], state_shift[:, i, :], ident[:, :]))
            wait(vector, m, fix_got)
            ad_f = ad_first[:, 0:1]
            sc = fix_s
            m = chain([
                lambda: vector.tensor_copy(sc[:, 0:1], fix[:, F + 1:W]),
                lambda: vector.tensor_copy(sc[:, 1:2], ps[6][:, 0:1]),
                lambda: vector.tensor_tensor(sc[:, 2:3], sc[:, 0:1], sc[:, 1:2], ALU.max),
                lambda: vector.tensor_copy(fix[:, F + 1:W], sc[:, 2:3]),
                lambda: vector.tensor_scalar(sc[:, 0:3], sc[:, 0:3], ad_f, None, ALU.add),
                lambda: vector.scalar_tensor_tensor(out=sc[:, 0:3], in0=sc[:, 0:3], scalar=SLOPE, in1=sc[:, 0:3], op0=ALU.mult, op1=ALU.max),
                lambda: vector.tensor_scalar(sc[:, 3:5], sc[:, 0:2], sc[:, 2:3], None, ALU.subtract),
            ])
            wait(scalar, m)
            m = act.after(scalar.activation(sc[:, 3:5], sc[:, 3:5], ACT.Exp))
            wait(vector, m)
            m = chain([
                lambda: vector.tensor_scalar(fix[:, 0:F + 1], fix[:, 0:F + 1], sc[:, 3:4], None, ALU.mult),
                lambda: vector.scalar_tensor_tensor(out=fix[:, 0:F], in0=ps[4][:, 0:F], scalar=sc[:, 4:5], in1=fix[:, 0:F],
                                                    op0=ALU.mult, op1=ALU.add),
                lambda: vector.scalar_tensor_tensor(out=fix[:, F:F + 1], in0=ps[5][:, 0:1], scalar=sc[:, 4:5], in1=fix[:, F:F + 1],
                                                    op0=ALU.mult, op1=ALU.add),
            ])
            wait(pool, m)
            fixed = stores["fix"].after(pool.indirect_dma_start(
                out=run_sum, out_offset=bass.IndirectOffsetOnAxis(ap=fix_i[:, :], axis=0), in_=fix[:, :], in_offset=None,
                bounds_check=P * L - 1, oob_is_err=False), 16)

            E = nodes(ring_a, W)
            wait(pool, fixed)
            gather_ends(run_sum, E)
            name = "c1" if layer == 0 else "c2"
            wait(scalar, h_stored)
            for b, (k0, k1) in enumerate(batches):
                wait(vector, ends_got[b])
                at = slice(k0, k1)
                end_top, own_top, top = s["s0"][:, at], s["s1"][:, at], s["rmax"][:, at]
                ad_n = s["ad"][:, at]

                def leaky(v):
                    return lambda: vector.scalar_tensor_tensor(out=v, in0=v, scalar=SLOPE, in1=v, op0=ALU.mult, op1=ALU.max)

                m = chain([
                    lambda: vector.tensor_tensor(end_top, E[:, at, F + 1], s["negE"][:, at], ALU.add),
                    lambda: vector.tensor_tensor(top, end_top, tab[:, at, F + 1], ALU.max),
                    lambda: vector.tensor_tensor(top, top, ad_n, ALU.add),
                    leaky(top),
                    lambda: vector.tensor_tensor(end_top, end_top, ad_n, ALU.add),
                    leaky(end_top),
                    lambda: vector.tensor_tensor(own_top, tab[:, at, F + 1], ad_n, ALU.add),
                    leaky(own_top),
                    lambda: vector.tensor_tensor(end_top, end_top, top, ALU.subtract),
                    lambda: vector.tensor_tensor(own_top, own_top, top, ALU.subtract),
                ])
                wait(scalar, m)
                act.after(scalar.activation(end_top, end_top, ACT.Exp))
                m = act.after(scalar.activation(own_top, own_top, ACT.Exp))
                wait(scalar, m)
                wait(vector, m)
                for k in range(k0, k1):
                    own = act.after(scalar.activation(tab[:, k, 0:F + 1], tab[:, k, 0:F + 1], ACT.Copy, scale=s["s1"][:, k:k + 1]))
                    wait(vector, own)
                    m = vec.after(vector.scalar_tensor_tensor(out=E[:, k, 0:F + 1], in0=E[:, k, 0:F + 1], scalar=s["s0"][:, k:k + 1],
                                                              in1=tab[:, k, 0:F + 1], op0=ALU.mult, op1=ALU.add))
                wait(vector, m)
                m = vec.after(vector.reciprocal(s["s3"][:, at], E[:, at, F]))
                wait(vector, m)
                for k in range(k0, k1):
                    m = vec.after(vector.scalar_tensor_tensor(out=E[:, k, 0:F], in0=E[:, k, 0:F], scalar=s["s3"][:, k:k + 1],
                                                              in1=bias[name][:, :], op0=ALU.mult, op1=ALU.add))
                if layer == 0:
                    ones_col = vec.after(vector.memset(tab[:, at, F:F + 1], 1.0))
                    wait(sync, ones_col)
                    new_h_stored, new_scattered = project(1, E, ACT.Relu, k0, k1, m)
                    continue
                wait(vector, m)
                m = vec.after(vector.scalar_tensor_tensor(out=x_sb[:, at, :], in0=E[:, at, 0:F], scalar=0.0,
                                                          in1=x_sb[:, at, :], op0=ALU.max, op1=ALU.add))
                wait(vector, m)
                m = layernorm(x_sb, k0, k1)
                wait(sync, m)
                k2 = min(k1, FULL)
                written = stores["out"].after(sync.dma_start(
                    out[k0 * P:k2 * P, :].rearrange("(k p) f -> p k f", p=P), x_sb[:, k0:k2, :]), 16)
                if k1 > FULL:
                    written = stores["out"].after(sync.dma_start(out[FULL * P:N, :], x_sb[0:REST, FULL, :]), 16)
            if layer == 0:
                h_stored, scattered, e_read = new_h_stored, new_scattered, m
        wait(sync, written)


_NAMES = {"x": "x", "srcT": "src", "src": "src", "srcL": "src", "dst": "dst", "W1": "L0_gnn_W1", "b1": "L0_gnn_b1", "W2": "L0_gnn_W2",
          "b2": "L0_gnn_b2", "W3": "L0_gnn_W3", "b3": "L0_gnn_b3", "C1": "L1_gnn_W1", "as1": "L1_gnn_att_src1",
          "ad1": "L1_gnn_att_dst1", "cb1": "L1_gnn_b1", "C2": "L1_gnn_W2", "as2": "L1_gnn_att_src2",
          "ad2": "L1_gnn_att_dst2", "cb2": "L1_gnn_b2"}


def kernel(**inputs):
    import numpy as np
    import concourse.bacc as bacc
    from concourse.bass_utils import run_bass_kernel_spmd

    N, F = inputs["x"].shape
    E = inputs["src"].shape[0]
    L = -(-E // 128)
    nc = bacc.Bacc("TRN2", target_bir_lowering=False, num_devices=1)
    arrays, aps = {}, {}
    for short, name in _NAMES.items():
        a = np.ascontiguousarray(inputs[name])
        if short in ("src", "srcT", "srcL", "dst"):
            a = np.concatenate([a, np.full(128 * L - E, N if short == "dst" else 0, a.dtype)]).reshape(128, L)
            if short == "srcT":
                a = np.ascontiguousarray(a.reshape(L, 128).T)
            if short == "srcL":
                a = np.ascontiguousarray(a.T)
        arrays[f"in_{short}"] = a
        aps[short] = nc.dram_tensor(f"in_{short}", a.shape, mybir.dt.from_np(a.dtype), kind="ExternalInput").ap()
    out = nc.dram_tensor("out", (N, F), F32, kind="ExternalOutput").ap()
    edge_network(nc, aps, out)
    result = run_bass_kernel_spmd(nc, [arrays], core_ids=[0])
    return result.results[0]["out"]
```

```python
from contextlib import ExitStack

import concourse.bass as bass
from concourse import mybir
from concourse.alu_op_type import AluOpType as ALU

F32 = mybir.dt.float32
I32 = mybir.dt.int32
BF16, I16 = mybir.dt.bfloat16, mybir.dt.int16
ACT = mybir.ActivationFunctionType
AX_X = mybir.AxisListType.X

P = 128
BIG = 1.0e30
SLOPE = 0.2
EPS = 1e-5


class Signal:

    def __init__(self, sem):
        self.sem, self.value = sem, 0

    def after(self, instruction, n=1):
        instruction.then_inc(self.sem, n)
        self.value += n
        return self.sem, self.value


def wait(engine, *marks):
    for sem, value in marks:
        engine.wait_ge(sem, value)


def cut(total, size, small):
    at, groups = 0, []
    while at < total:
        step = size if total - at >= size + small else min(small, total - at)
        groups.append((at, at + step))
        at += step
    return groups


def edge_network(nc, t, out):
    N, F = t["x"].shape
    L = t["src"].shape[1]
    NB = -(-N // P)
    NP = NB * P
    CHUNKS = L
    FULL, REST = N // P, N % P
    G, RING, AHEAD = 8, 6, 4
    G1, RING1, PIECE = 10, 3, 7
    LAST_PIECE = (NB - 1) // PIECE
    W = F + 2
    batches = [(k, min(k + 7, NB)) for k in range(0, NB, 7)]
    groups, groups1 = cut(L, G, 4), cut(L, G1, 5)
    vector, scalar, tensor, pool, sync = nc.vector, nc.scalar, nc.tensor, nc.gpsimd, nc.sync

    CB = -(-CHUNKS // P)
    BL = CB * P
    WINDOWS = NP + P
    P_compact = nc.dram_tensor("P_compact", (WINDOWS, F), F32).ap()
    rank_rows = nc.dram_tensor("rank_rows", (2, P * BL), BF16).ap()
    first_ranks = nc.dram_tensor("first_ranks", (1, P * CB), I32).ap()
    Q_table = nc.dram_tensor("Q_table", (NP, F), F32).ap()
    H_table = nc.dram_tensor("H_table", (NP, W), F32).ap()
    run_max = nc.dram_tensor("run_max", (P * L, F), F32).ap()
    run_sum = nc.dram_tensor("run_sum", (P * L, W), F32).ap()
    bounds_table = nc.dram_tensor("bounds_table", (NP, 2), F32).ap()
    ad_edges = nc.dram_tensor("ad_edges", (P * L, 1), F32).ap()

    with ExitStack() as ctx:
        def sb(name, shape, dt=F32):
            return ctx.enter_context(nc.sbuf_tensor(name, shape, dt))

        def signal(name):
            return Signal(ctx.enter_context(nc.semaphore(name)))

        def nodes(flat, width):
            return flat[:, 0:NB * width].rearrange("p (k f) -> p k f", f=width)

        ident, tri, ones = sb("ident", [P, P]), sb("tri", [P, P]), sb("ones", [P, P])
        shift, wrap, iota_row = sb("shift", [P, P]), sb("wrap", [P, P]), sb("iota_row", [P, P])
        iota_i, iota_col_i = sb("iota_i", [P, P], I32), sb("iota_col_i", [P, 1], I32)
        next_i, next_n = sb("next_i", [P, NB], I32), sb("next_n", [P, NB])
        code_bias = sb("code_bias", [P, LAST_PIECE + 1])
        code, block_at = sb("code", [P, LAST_PIECE + 1, P], I16), sb("block_at", [P, PIECE, P], I16)
        block_at_i = sb("block_at_i", [P, PIECE], I32)
        src_row = sb("src_row", [P, 2, P], I32)
        x_sb = sb("x_sb", [P, NB, F])
        work = sb("work", [P, NP + 7 * 512])
        turned = work[:, 0:NP]
        split = work[:, :].bitcast(BF16)[:, 0:NB * 3 * W].rearrange("p (k s f) -> p k s f", s=3, f=W)
        tab_flat = sb("tab_flat", [P, NB * W])
        tab = tab_flat[:, :].rearrange("p (k f) -> p k f", f=W)
        ring_a, ring_b = sb("ring_a", [P, NB * W]), sb("ring_b", [P, NB * W])
        src_i, dst_i = sb("src_i", [P, L], I32), sb("dst_i", [P, L], I32)
        srcT_i = src_i
        neg_wide, ad_wide = sb("neg_wide", [P, BL]), sb("ad_wide", [P, BL])
        neg, ad_exp = neg_wide[:, 0:L], ad_wide[:, 0:L]
        chunk_dst, rank = ad_wide[:, :].bitcast(I32), neg_wide
        pair = sb("pair", [P, 2, BL], BF16)
        fresh = ring_b[:, 0:BL]
        before = sb("before", [P, 1], I32)
        first_rank, first_rank_i = sb("first_rank", [P, CB]), sb("first_rank_i", [P, CB], I32)
        total, iota_col = sb("total", [P, 2]), sb("iota_col", [P, 1])
        first_row = pair[0:1, :, :].rearrange("p s l -> p (s l)").bitcast(I32)
        onto, scanned, m1T = (work[:, NP + a * 512:NP + b * 512].rearrange("p (s e) -> p s e", e=512)
                              for a, b in ((0, 3), (3, 5), (5, 7)))
        weights = {n: sb(n, [P, w]) for n, w in (
            ("W1", F), ("W2a", F), ("W2b", F), ("Wpq", 2 * F), ("W3", F), ("Wt", F))}
        conv_w = [sb(f"conv_w{c}", [P, W]) for c in range(2)]
        b1_col = sb("b1_col", [P, 1])
        att_cols = [sb(f"att{c}", [P, 2]) for c in range(2)]
        bias = {n: sb(n + "_rows", [P, F]) for n in ("b2", "b3", "c1", "c2")}
        cf_i, cf_part = sb("cf_i", [P, CB], I32), sb("cf_part", [P, 2, CB], I32)
        cf_f = sb("cf_f", [P, 2, CB])
        onehot = sb("onehot", [P, 2, P])
        small = {n: sb(n, [P, NB]) for n in (
            "cnt", "base", "cfle", "row_f", "ends", "starts", "empty", "negE", "s0", "s3",
            "rstd", "centre", "ad", "ad_end")}
        row_i, end_i, start_i, place_i = (sb(n, [P, NB], I32) for n in ("row_i", "end_i", "start_i", "place_i"))
        zero_wide = sb("zero_wide", [P, L // 3])
        zero_tile = zero_wide[:, 0:W]
        assert L % 3 == 0
        rows = {n: sb("r_" + n, [P, P]) for n in ("dfirst", "dlast", "link", "adl", "rs", "ma", "ms", "l", "cc")}
        state, state_shift = sb("state", [P, P]), sb("state_shift", [P, 3, P])
        fix, fix_s, fix_i = sb("fix", [P, W]), sb("fix_s", [P, 5]), sb("fix_i", [P, 1], I32)
        first_start_i, first_bounds = sb("first_start_i", [P, 1], I32), sb("first_bounds", [P, 2])
        bounds_sb, fix_f = sb("bounds_sb", [P, NB, 2]), sb("fix_f", [P, 3])
        two = sb("two", [P, 2, NB])
        stats, moments = sb("stats", [P, NB, 6]), sb("moments", [P, NB, 2])
        dcol = sb("dcol", [P, 2])
        gz, gd, gw = (sb(n, [P, G1]) for n in ("gz", "gd", "gw"))
        gmm = sb("gmm", [P, 2, G1 + 1])
        ge, gc = sb("ge", [P, 2, G1]), sb("gc", [P, 2, G1])
        ad_first = sb("ad_first", [P, 1])
        ps = [ctx.enter_context(nc.psum_tensor(f"ps{i}", [P, 512], F32)) for i in range(8)]

        vec, act, pe, gp = signal("vec"), signal("act"), signal("pe"), signal("gp")
        loads = {n: signal("ld_" + n) for n in ("x", "w", "edges", "cf", "chunks", "firsts", "srcT", "fix", "ad", "adx")}
        stores = {n: signal("st_" + n) for n in ("tabs", "compact0", "pscatter", "ranks", "h", "bounds", "fix", "zero", "adscatter", "out")}
        q_sem = [signal(f"q_slot{i}") for i in range(RING)]
        w_sem = [signal(f"w_slot{i}") for i in range(RING)]
        b_sem = [signal(f"b_slot{i}") for i in range(RING)]
        node_sem = [signal(f"nodes{i}") for i in range(len(batches))]
        ends_got = {}
        row_sem = [signal(f"src_row{i}") for i in range(2)]
        s_sem = [signal(f"s_slot{i}") for i in range(RING)]

        flat = t["dst"].rearrange("p l -> (p l)")
        flat_dst = flat.rearrange("(c e) -> c e", e=P)
        padded = gp.after(pool.memset(cf_i[:, :], NP + P))
        wait(sync, padded)
        with nc.allow_non_contiguous_dma(reason="one value of every 128, once"):
            whole = CHUNKS // P
            loads["cf"].after(sync.dma_start(cf_i[:, 0:whole], flat_dst[0:whole * P, 0:1].rearrange("(k p) a -> p (k a)", p=P)), 16)
            cf_ready = loads["cf"].after(sync.dma_start(cf_i[0:CHUNKS - whole * P, whole:whole + 1], flat_dst[whole * P:CHUNKS, 0:1]), 16)
        for m, value in ((ident, 0.0), (ones, 1.0), (tri, 1.0), (shift, 0.0), (wrap, 0.0), (zero_wide, 0.0)):
            made = gp.after(pool.memset(m[:, :], value))
        wait(pool, made)
        for m, op, fill, base, step, cm in ((ident, ALU.not_equal, 1.0, 0, -1, 1), (tri, ALU.is_ge, 0.0, 0, 1, -1),
                                            (shift, ALU.not_equal, 1.0, 1, -1, 1), (wrap, ALU.not_equal, 1.0, 1 - P, -1, 1)):
            gp.after(pool.affine_select(out=m[:, :], in_=m[:, :], compare_op=op, fill=fill, base=base,
                                        pattern=[[step, P]], channel_multiplier=cm))
        gp.after(pool.iota(iota_i[:, :], pattern=[[1, P]], base=0, channel_multiplier=0))
        gp.after(pool.iota(iota_col_i[:, :], pattern=[[0, 1]], base=0, channel_multiplier=1))
        gp.after(pool.iota(block_at_i[:, :], pattern=[[P, PIECE]], base=0, channel_multiplier=0))
        consts = gp.after(pool.iota(next_i[:, :], pattern=[[P, NB]], base=1, channel_multiplier=1))
        gp.after(pool.memset(x_sb[:, NB - 1, :], 0.0))
        gp.after(pool.memset(chunk_dst, N))
        blank = gp.after(pool.memset(before[:, :], -1))

        wait(sync, blank)
        x_in = t["x"][0:FULL * P, :].rearrange("(k p) f -> p k f", p=P)
        loads["x"].after(sync.dma_start(x_sb[:, 0:FULL, :], x_in), 16)
        x_ready = loads["x"].after(sync.dma_start(x_sb[0:REST, FULL, :], t["x"][FULL * P:N, :]), 16)
        full, rest = P * L // BL, P * L % BL
        loads["chunks"].after(sync.dma_start(chunk_dst[0:full, :], flat[0:full * BL].rearrange("(p l) -> p l", l=BL)), 16)
        loads["chunks"].after(sync.dma_start(chunk_dst[full:full + 1, 0:rest], flat[full * BL:].rearrange("(a l) -> a l", a=1)), 16)
        with nc.allow_non_contiguous_dma(reason="one value for each partition, once"):
            chunks_ready = loads["chunks"].after(sync.dma_start(
                before[1:full + 1, :], flat[0:full * BL].rearrange("(p l) -> p l", l=BL)[:, BL - 1:BL]), 16)
        srcT_ready = loads["srcT"].after(sync.dma_start(srcT_i[:, :], t["srcT"]), 16)
        edges_ready = loads["edges"].after(sync.dma_start(dst_i[:, :], t["dst"]), 16)
        ld = loads["w"]
        W2 = t["W2"]

        def column(name):
            return t[name].rearrange("(p a) -> p a", a=1)

        for dst, srcap in (
            (weights["W1"][:, :], t["W1"]), (b1_col[:, :], column("b1")),
            (weights["W2a"][:, :], W2[0:F, :]), (weights["W2b"][:, :], W2[F:2 * F, :]),
            (bias["b2"][:, :], t["b2"].rearrange("(a f) -> a f", a=1).broadcast_to([P, F])),
            (weights["W3"][:, :], t["W3"]), (conv_w[0][:, 0:F], t["C1"]), (conv_w[1][:, 0:F], t["C2"]),
            (att_cols[0][:, 0:1], column("as1")), (att_cols[0][:, 1:2], column("ad1")),
            (att_cols[1][:, 0:1], column("as2")), (att_cols[1][:, 1:2], column("ad2")),
        ) + tuple((bias[n][:, :], t[k].rearrange("(a f) -> a f", a=1).broadcast_to([P, F]))
                  for n, k in (("b3", "b3"), ("c1", "cb1"), ("c2", "cb2"))):
            w_ready = ld.after(scalar.dma_start(dst, srcap), 16)
        wait(scalar, made)
        compact_zeroed = stores["compact0"].after(scalar.dma_start(
            P_compact.rearrange("(k p) f -> p k f", p=P), zero_tile[:, 0:F].unsqueeze(1).to_broadcast([P, WINDOWS // P, F])), 16)

        zero_stored = stores["zero"].after(scalar.dma_start(
            ad_edges.rearrange("(p c l) a -> p c (l a)", p=P, c=3), zero_wide[:, 0:L // 3].unsqueeze(1).to_broadcast([P, 3, L // 3])), 16)
        wait(vector, consts, cf_ready)
        vec.after(vector.tensor_copy(iota_row[:, :], iota_i[:, :]))
        vec.after(vector.tensor_copy(next_n[:, :], next_i[:, :]))
        vec.after(vector.tensor_copy(block_at[:, :, :], block_at_i[:, :].unsqueeze(2).to_broadcast([P, PIECE, P])))
        for c in range(LAST_PIECE + 1):
            vec.after(vector.tensor_scalar(code_bias[:, c:c + 1], iota_col_i[:, :], -1.0, float(-c * PIECE * P), ALU.mult, ALU.add))
        vec.after(vector.tensor_copy(iota_col[:, :], iota_col_i[:, :]))
        vec.after(vector.tensor_scalar(cf_part[:, 0, :], cf_i[:, :], P - 1, None, ALU.bitwise_and))
        m = vec.after(vector.tensor_scalar(cf_part[:, 1, :], cf_i[:, :], 7, None, ALU.logical_shift_right))
        wait(vector, m)
        m = vec.after(vector.tensor_copy(cf_f[:, :, :], cf_part[:, :, :]))

        used = None
        for k in range(CB):
            wait(vector, m, *([used] if used else []))
            vec.after(vector.tensor_scalar(onehot[:, 0, :], iota_row[:, :], cf_f[:, 0, k:k + 1], None, ALU.is_equal))
            hot = vec.after(vector.tensor_scalar(onehot[:, 1, 0:NB], iota_row[:, 0:NB], cf_f[:, 1, k:k + 1], None, ALU.is_equal))
            wait(tensor, hot)
            used = pe.after(tensor.matmul(ps[0][:, 0:NB], lhsT=onehot[:, 0, :], rhs=onehot[:, 1, 0:NB],
                                          start=(k == 0), stop=(k == CB - 1)))
        wait(vector, used)
        m = vec.after(vector.tensor_copy(small["cnt"][:, :], ps[0][:, 0:NB]))

        def count_up(o, values, ready):
            wait(tensor, ready)
            pe.after(tensor.matmul(ps[1][:, 0:NB], lhsT=tri[:, :], rhs=values, start=True, stop=True))
            m = pe.after(tensor.matmul(ps[2][:, 0:NB], lhsT=ones[:, :], rhs=values, start=True, stop=True))
            wait(vector, m)
            m = vec.after(vector.tensor_copy(small["s0"][:, :], ps[2][:, 0:NB]))
            wait(vector, m)
            m = vec.after(vector.tensor_tensor_scan(small["base"][:, :], ones[:, 0:NB], small["s0"][:, :], 0.0, ALU.mult, ALU.add))
            wait(vector, m)
            m = vec.after(vector.tensor_tensor(small["base"][:, :], small["base"][:, :], small["s0"][:, :], ALU.subtract))
            wait(vector, m)
            return vec.after(vector.tensor_tensor(o, ps[1][:, 0:NB], small["base"][:, :], ALU.add))

        m = count_up(small["cfle"][:, :], small["cnt"][:, :], m)
        wait(vector, m)
        m = vec.after(vector.tensor_scalar(small["row_f"][:, :], small["cfle"][:, :], -1.0, 0.0, ALU.add, ALU.max))
        wait(vector, m)
        m = vec.after(vector.tensor_copy(row_i[:, :], small["row_f"][:, :]))
        wait(pool, m)
        dst_rows = ring_a[:, :].bitcast(I32)[:, 0:NP].rearrange("p (k e) -> p k e", e=P)
        rows_got = {}
        for b, (k0, k1) in enumerate(batches):
            for k in range(k0, k1):
                rows_got[b] = node_sem[b].after(pool.indirect_dma_start(
                    out=dst_rows[:, k, :], out_offset=None, in_=flat_dst,
                    in_offset=bass.IndirectOffsetOnAxis(ap=row_i[:, k:k + 1], axis=0)), 16)
        wait(vector, chunks_ready)
        vec.after(vector.tensor_tensor(fresh[:, 1:BL], chunk_dst[:, 1:BL], chunk_dst[:, 0:BL - 1], ALU.not_equal))
        m2 = vec.after(vector.tensor_tensor(fresh[:, 0:1], chunk_dst[:, 0:1], before[:, :], ALU.not_equal))
        wait(vector, m2)
        vec.after(vector.tensor_scalar(pair[:, 1, :], fresh[:, :], -BIG, None, ALU.mult))
        m2 = vec.after(vector.tensor_tensor_scan(rank[:, :], ones[:, 0:1].to_broadcast([P, BL]), fresh[:, :], 0.0, ALU.mult, ALU.add))
        wait(vector, m2)
        m2 = vec.after(vector.tensor_copy(total[:, 0:1], rank[:, BL - 1:BL]))
        wait(tensor, m2)
        m2 = pe.after(tensor.matmul(ps[3][:, 0:1], lhsT=tri[:, :], rhs=total[:, 0:1], start=True, stop=True))
        wait(vector, m2)
        m2 = vec.after(vector.tensor_tensor(total[:, 1:2], ps[3][:, 0:1], total[:, 0:1], ALU.subtract))
        wait(vector, m2)
        firsts = rank[:, :].rearrange("p (c e) -> p c e", e=P)[:, :, 0]
        m2 = vec.after(vector.tensor_copy(first_rank[:, :], firsts))
        wait(vector, m2)
        vec.after(vector.tensor_tensor(pair[:, 0, :].rearrange("p (c e) -> p c e", e=P), rank[:, :].rearrange("p (c e) -> p c e", e=P),
                                       first_rank[:, :].unsqueeze(2).to_broadcast([P, CB, P]), ALU.subtract))
        m2 = vec.after(vector.tensor_scalar(first_rank_i[:, :], first_rank[:, :], total[:, 1:2], -1.0, ALU.add, ALU.add))
        wait(sync, m2)
        stores["ranks"].after(sync.dma_start(rank_rows.rearrange("s (p l) -> p s l", p=P), pair[:, :, :]), 16)
        ranks_stored = stores["ranks"].after(sync.dma_start(first_ranks.rearrange("a (p c) -> p (a c)", p=P), first_rank_i[:, :]), 16)
        wait(sync, ranks_stored)
        firsts_ready = loads["firsts"].after(sync.dma_start(first_row[:, :], first_ranks), 16)

        def turn(source, ready):
            wait(tensor, ready)
            free = {}
            for q, k0 in enumerate(range(0, NB, 4)):
                bank, ks = ps[6 + q % 2], range(k0, min(k0 + 4, NB))
                if q % 2 in free:
                    wait(tensor, free[q % 2])
                for k in ks:
                    mark = pe.after(tensor.transpose(bank[:, (k - k0) * P:(k - k0 + 1) * P], source[:, k, 0:F], ident[:, :]))
                wait(scalar, mark)
                n = len(ks) * P
                free[q % 2] = act.after(scalar.activation(turned[:, k0 * P:k0 * P + n], bank[:, 0:n], ACT.Copy))
            return free[q % 2]

        wait(vector, w_ready)
        vec.after(vector.tensor_tensor(weights["Wpq"][:, 0:F], weights["W2a"][:, :], weights["W2b"][:, :], ALU.subtract))
        folded = vec.after(vector.tensor_copy(weights["Wpq"][:, F:2 * F], weights["W2b"][:, :]))

        turned_x = turn(x_sb, x_ready)
        wait(tensor, w_ready, turned_x, folded)
        free = {}
        for q, c0 in enumerate(range(0, NP, 512)):
            n = min(512, NP - c0)
            b = 2 + q % 2
            if b in free:
                wait(tensor, free[b])
            mark = pe.after(tensor.matmul(ps[b][:, 0:n], lhsT=weights["W1"][:, :], rhs=turned[:, c0:c0 + n], start=True, stop=True))
            wait(scalar, mark)
            free[b] = act.after(scalar.activation(turned[:, c0:c0 + n], ps[b][:, 0:n], ACT.Identity, bias=b1_col[:, 0:1]))
        h_ready = free[b]
        wait(tensor, h_ready, folded)
        below = ring_a[:, 0:NP].rearrange("p (k e) -> p k e", e=P)

        def count_rows(b):
            k0, k1 = batches[b]
            wait(vector, rows_got[b])
            m = vec.after(vector.tensor_tensor(below[:, k0:k1, :], dst_rows[:, k0:k1, :],
                                               next_n[:, k0:k1].unsqueeze(2).to_broadcast([P, k1 - k0, P]), ALU.is_lt))
            wait(vector, m)
            return vec.after(vector.tensor_reduce(small["s0"][:, k0:k1], below[:, k0:k1, :], AX_X, ALU.add))

        p_stage, q_stage = nodes(tab_flat, F), nodes(ring_b, F)
        free = {}
        for q, k0 in enumerate(range(0, NB, 2)):
            ks = range(k0, min(k0 + 2, NB))
            b = 4 + q % 4
            if b in free:
                wait(tensor, free[b])
            for i, k in enumerate(ks):
                mark = pe.after(tensor.matmul(ps[b][:, i * 256:(i + 1) * 256], lhsT=turned[:, k * P:(k + 1) * P],
                                              rhs=weights["Wpq"][:, :], start=True, stop=True))
            wait(vector, mark)
            n = len(ks)
            both = ps[b][:, 0:n * 256].rearrange("p (k s f) -> p k s f", s=2, f=F)
            p_free = vec.after(vector.tensor_tensor(p_stage[:, k0:k0 + n, :], both[:, :, 0, :],
                                                    bias["b2"][:, :].unsqueeze(1).to_broadcast([P, n, F]), ALU.add))
            wait(scalar, mark, p_free)
            free[b] = act.after(scalar.activation(q_stage[:, k0:k0 + n, :], both[:, :, 1, :], ACT.Copy))
            if q % 4 == 3 and q // 4 < len(batches) - 1:
                counted = count_rows(q // 4)
        pq_ready, p_ready = free[b], p_free
        wait(sync, pq_ready)
        tables_stored = stores["tabs"].after(sync.dma_start(Q_table.rearrange("(k p) f -> p k f", p=P), q_stage), 16)

        m = counted = count_rows(len(batches) - 1)
        wait(vector, m)
        m = vec.after(vector.scalar_tensor_tensor(out=small["ends"][:, :], in0=small["row_f"][:, :], scalar=float(P),
                                                  in1=small["s0"][:, :], op0=ALU.mult, op1=ALU.add))
        wait(tensor, m)
        tensor.matmul(ps[1][:, 0:NB], lhsT=shift[:, :], rhs=small["ends"][:, :], start=True, stop=False)
        m = pe.after(tensor.matmul(ps[1][:, 1:NB], lhsT=wrap[:, :], rhs=small["ends"][:, 0:NB - 1], start=False, stop=True))
        wait(vector, m)
        m = vec.after(vector.tensor_copy(small["starts"][:, :], ps[1][:, 0:NB]))
        wait(vector, m)
        s = small

        def chain(instructions):
            mark = None
            for make in instructions:
                mark = vec.after(make())
                wait(vector, mark)
            return mark

        index_ready = chain([
            lambda: vector.tensor_tensor(s["empty"][:, :], s["ends"][:, :], s["starts"][:, :], ALU.is_equal),
            lambda: vector.tensor_scalar(s["negE"][:, :], s["empty"][:, :], -BIG, None, ALU.mult),
            lambda: vector.scalar_tensor_tensor(out=s["s0"][:, :], in0=s["empty"][:, :], scalar=1.0e6, in1=s["starts"][:, :],
                                                op0=ALU.mult, op1=ALU.add),
            lambda: vector.tensor_copy(start_i[:, :], s["s0"][:, :]),
            lambda: vector.tensor_scalar(s["s0"][:, :], s["ends"][:, :], -1.0, 0.0, ALU.add, ALU.max),
            lambda: vector.tensor_copy(end_i[:, :], s["s0"][:, :]),
            lambda: vector.tensor_scalar(s["cnt"][:, :], s["empty"][:, :], -1.0, 1.0, ALU.mult, ALU.add),
        ])
        m = count_up(s["s3"][:, :], s["cnt"][:, :], index_ready)
        wait(vector, m)
        rank_index = chain([
            lambda: vector.scalar_tensor_tensor(out=s["s3"][:, :], in0=s["empty"][:, :], scalar=1.0e6, in1=s["s3"][:, :],
                                                op0=ALU.mult, op1=ALU.add),
            lambda: vector.tensor_scalar(s["s3"][:, :], s["s3"][:, :], -1.0, None, ALU.add),
            lambda: vector.tensor_copy(place_i[:, :], s["s3"][:, :]),
        ])
        wait(vector, ranks_stored)
        m2 = vec.after(vector.tensor_tensor(neg[:, 1:L], dst_i[:, 1:L], dst_i[:, 0:L - 1], ALU.not_equal))
        vec.after(vector.memset(neg[:, 0:1], -BIG))
        wait(vector, m2)
        vec.after(vector.tensor_scalar(neg[:, 1:L], neg[:, 1:L], -BIG, None, ALU.mult))
        vec.after(vector.tensor_copy(dcol[:, 0:1], dst_i[:, 0:1]))
        dcol_ready = vec.after(vector.tensor_copy(dcol[:, 1:2], dst_i[:, L - 1:L]))


        def spread(column, bank):
            return pe.after(tensor.matmul(bank, lhsT=column.to_broadcast([P, P]), rhs=ident[:, :], start=True, stop=True))

        vec.after(vector.tensor_copy(bounds_sb[:, :, 0], s["starts"][:, :]))
        m = vec.after(vector.tensor_copy(bounds_sb[:, :, 1], s["ends"][:, :]))
        wait(sync, m)
        bounds_stored = stores["bounds"].after(sync.dma_start(bounds_table.rearrange("(k p) a -> p k a", p=P), bounds_sb[:, :, :]), 16)
        wait(tensor, dcol_ready, rank_index)
        spread(dcol[:, 0:1], ps[0][:, 0:P])
        m = spread(dcol[:, 1:2], ps[1][:, 0:P])
        wait(vector, m)
        r = rows
        vec.after(vector.tensor_copy(r["dfirst"][:, :], ps[0][:, 0:P]))
        chain([
            lambda: vector.tensor_copy(r["dlast"][:, :], ps[1][:, 0:P]),
            lambda: vector.memset(r["link"][:, :], 0.0),
            lambda: vector.tensor_tensor(r["link"][:, 1:P], r["dfirst"][:, 1:P], r["dlast"][:, 0:P - 1], ALU.is_equal),
            lambda: vector.tensor_tensor(r["cc"][:, :], r["dfirst"][:, :], r["dlast"][:, :], ALU.is_equal),
            lambda: vector.tensor_tensor(r["link"][:, :], r["link"][:, :], r["cc"][:, :], ALU.mult),
        ])
        chain([lambda: vector.tensor_scalar(r["link"][:, :], r["link"][:, :], -1.0, BIG, ALU.add, ALU.mult)])

        q_ring = ring_a[:, 0:RING * G * F].rearrange("p (s g f) -> p s g f", s=RING, f=F)
        w_ring = turned[:, 0:RING * G * F].rearrange("p (s g f) -> p s g f", s=RING, f=F)
        b_ring = tab_flat[:, :].bitcast(BF16)[:, 0:RING * 2 * G * P].rearrange("p (s r e) -> p s r e", s=RING, r=2)
        o_ring = ring_b[:, 0:RING * G * F].rearrange("p (s g f) -> p s g f", s=RING, f=F)
        quads = [(g, a, min(4, j1 - j0 - a)) for g, (j0, j1) in enumerate(groups) for a in range(0, j1 - j0, 4)]
        last_of = {g: i for i, (g, a, n) in enumerate(quads)}
        placed, relued, multiplied, scan_done, turned_back, evacuated, stored = {}, {}, {}, {}, {}, {}, {}
        gathered, windowed, hot = {}, {}, {}

        def gather_q(g):
            j0, j1 = groups[g]
            slot = g % RING
            if g >= RING:
                wait(pool, placed[last_of[g - RING]])
            for j in range(j0, j1):
                gathered[g] = q_sem[slot].after(pool.indirect_dma_start(
                    out=q_ring[:, slot, j - j0, :], out_offset=None, in_=Q_table,
                    in_offset=bass.IndirectOffsetOnAxis(ap=srcT_i[:, j:j + 1], axis=0)), 16)

        def load_windows(g):
            j0, j1 = groups[g]
            slot = g % RING
            if g >= RING:
                wait(sync, placed[last_of[g - RING]], scan_done[last_of[g - RING]])
            b = b_sem[slot].after(sync.dma_start(
                b_ring[:, slot, :, 0:(j1 - j0) * P],
                rank_rows[:, j0 * P:j1 * P].unsqueeze(0).to_broadcast([P, 2, (j1 - j0) * P])), 16)
            for j in range(j0, j1, 4):
                n = min(4, j1 - j)
                _, at = nc.values_load_multi_w_load_instructions(first_row[0:1, j:j + n], engines=[sync.engine],
                                                                 min_val=0, max_val=WINDOWS - P)
                for i in range(n):
                    w = w_sem[slot].after(sync.dma_start(w_ring[:, slot, j + i - j0, :], P_compact[bass.ds(at[i], P), :]), 16)
            windowed[g] = (w, b)

        def spread_ranks(i):
            g, a, n = quads[i]
            if i >= 3:
                wait(vector, placed[i - 3])
            wait(vector, windowed[g][1])
            hot[i] = vec.after(vector.tensor_scalar(onto[:, i % 3, 0:n * P], b_ring[:, g % RING, 0, a * P:(a + n) * P],
                                                    iota_col[:, 0:1], None, ALU.is_equal))

        def stage_a(i):
            g, a, n = quads[i]
            b = i % 2
            if i >= 2:
                wait(tensor, relued[i - 2])
            wait(tensor, gathered[g], windowed[g][0], hot[i])
            for c in range(n):
                piece = ps[b][:, c * P:(c + 1) * P]
                pe.after(tensor.matmul(piece, lhsT=q_ring[:, g % RING, a + c, :], rhs=ident[:, :], start=True, stop=False))
                placed[i] = pe.after(tensor.matmul(piece, lhsT=w_ring[:, g % RING, a + c, :], rhs=onto[:, i % 3, c * P:(c + 1) * P],
                                                   start=False, stop=True))
            if i >= 2:
                wait(scalar, multiplied[i - 2])
            wait(scalar, placed[i])
            relued[i] = act.after(scalar.activation(m1T[:, b, 0:n * P], ps[b][:, 0:n * P], ACT.Relu))

        def stage_b(i):
            g, a, n = quads[i]
            b = i % 2
            if i >= 2:
                wait(tensor, scan_done[i - 2])
            wait(tensor, relued[i])
            multiplied[i] = pe.after(tensor.matmul(ps[2 + b][:, 0:n * P], lhsT=weights["W3"][:, :], rhs=m1T[:, b, 0:n * P],
                                                   start=True, stop=True))
            if i >= 2:
                wait(vector, turned_back[i - 2])
            if i >= 1:
                wait(vector, scan_done[i - 1])
            wait(vector, multiplied[i])
            initial = scanned[:, 1 - b, quads[i - 1][2] * P - 1:quads[i - 1][2] * P] if i else 0.0
            scan_done[i] = vec.after(vector.tensor_tensor_scan(
                scanned[:, b, 0:n * P], b_ring[:, g % RING, 1, a * P:(a + n) * P], ps[2 + b][:, 0:n * P], initial, ALU.add, ALU.max))

        def stage_c(i):
            g, a, n = quads[i]
            b, slot = i % 2, g % RING
            if i >= 2:
                wait(tensor, evacuated[i - 2])
            wait(tensor, scan_done[i])
            for c in range(n):
                turned_back[i] = pe.after(tensor.transpose(ps[4 + b][:, c * P:(c + 1) * P], scanned[:, b, c * P:(c + 1) * P], ident[:, :]))
            if a == 0 and g >= RING:
                wait(scalar, stored[g - RING])
            wait(scalar, turned_back[i])
            evacuated[i] = act.after(scalar.activation(o_ring[:, slot, a:a + n, :],
                                                       ps[4 + b][:, 0:n * P].rearrange("p (c f) -> p c f", f=F), ACT.Copy))
            if i == last_of[g]:
                j0, j1 = groups[g]
                wait(sync, evacuated[i])
                stored[g] = s_sem[slot].after(sync.dma_start(
                    run_max.rearrange("(c p) f -> p c f", p=P)[:, j0:j1, :], o_ring[:, slot, 0:j1 - j0, :]), 16)

        wait(pool, srcT_ready, tables_stored, counted)
        gather_q(0)
        gather_q(1)
        wait(pool, p_ready, rank_index, compact_zeroed)
        for k in range(NB):
            p_scattered = stores["pscatter"].after(pool.indirect_dma_start(
                out=P_compact, out_offset=bass.IndirectOffsetOnAxis(ap=place_i[:, k:k + 1], axis=0),
                in_=p_stage[:, k, :], in_offset=None, bounds_check=WINDOWS - 1, oob_is_err=False), 16)

        wait(pool, bounds_stored, edges_ready)
        bounds_got = loads["fix"].after(pool.indirect_dma_start(
            out=first_bounds[:, :], out_offset=None, in_=bounds_table,
            in_offset=bass.IndirectOffsetOnAxis(ap=dst_i[:, 0:1], axis=0)), 16)

        wait(sync, p_scattered, firsts_ready, pq_ready)
        wait(scalar, tables_stored)
        for g in range(AHEAD):
            load_windows(g)
        wait(vector, bounds_got)
        b0, b1 = first_bounds[:, 0:1], first_bounds[:, 1:2]
        chain([
            lambda: vector.tensor_copy(first_start_i[:, :], b0),
            lambda: vector.tensor_scalar(fix_f[:, 2:3], iota_col[:, :], float(L), None, ALU.mult),
            lambda: vector.tensor_tensor(fix_f[:, 0:1], b0, fix_f[:, 2:3], ALU.is_ge),
            lambda: vector.tensor_scalar(fix_f[:, 1:2], b1, float(L), None, ALU.subtract),
            lambda: vector.tensor_tensor(fix_f[:, 1:2], fix_f[:, 1:2], fix_f[:, 2:3], ALU.is_gt),
            lambda: vector.tensor_tensor(fix_f[:, 0:1], fix_f[:, 0:1], fix_f[:, 1:2], ALU.max),
            lambda: vector.scalar_tensor_tensor(out=fix_f[:, 0:1], in0=fix_f[:, 0:1], scalar=1.0e6, in1=b1, op0=ALU.mult, op1=ALU.add),
            lambda: vector.tensor_scalar(fix_f[:, 0:1], fix_f[:, 0:1], -1.0, None, ALU.add),
            lambda: vector.tensor_copy(fix_i[:, :], fix_f[:, 0:1]),
        ])
        w_made = {}
        for layer in range(2):
            w = conv_w[layer]
            wait(tensor, w_ready, pq_ready)
            m = pe.after(tensor.transpose(ps[6][:, 0:P], w[:, 0:F], ident[:, :]))
            wait(vector, m)
            m = vec.after(vector.tensor_copy(weights["Wt"][:, :], ps[6][:, 0:P]))
            wait(tensor, m)
            m = pe.after(tensor.matmul(ps[7][:, 0:2], lhsT=weights["Wt"][:, :], rhs=att_cols[layer][:, :], start=True, stop=True))
            wait(vector, m)
            w_made[layer] = vec.after(vector.tensor_copy(w[:, F:W], ps[7][:, 0:2]))
        spread_ranks(0)
        for i in range(len(quads) + 2):
            if i < len(quads):
                g, a, n = quads[i]
                if a == 0 and g >= 2:
                    gather_q(g)
                stage_a(i)
            if i + 1 < len(quads):
                spread_ranks(i + 1)
            if 0 <= i - 1 < len(quads):
                stage_b(i - 1)
            if i < len(quads) and a == 0 and g + AHEAD < len(groups):
                load_windows(g + AHEAD)
            if i >= 2:
                stage_c(i - 2)
        last_quad = len(quads) - 1

        def over(small_ap, width):
            return small_ap.unsqueeze(2).to_broadcast([P, small_ap.shape[1], width])

        def gather_ends(table, view, b):
            for k in range(*batches[b]):
                ends_got[b] = node_sem[b].after(pool.indirect_dma_start(
                    out=view[:, k, :], out_offset=None, in_=table,
                    in_offset=bass.IndirectOffsetOnAxis(ap=end_i[:, k:k + 1], axis=0)), 16)

        def spread_of(y, k0, k1):
            for k in range(k0, k1):
                m = vec.after(vector.bn_stats(stats[:, k, :], y[:, k, :]))
            wait(vector, m)
            for k in range(k0, k1):
                m = vec.after(vector.bn_aggr(moments[:, k, :], stats[:, k, :]))
            wait(vector, m)
            return vec.after(vector.tensor_scalar(s["rstd"][:, k0:k1], moments[:, k0:k1, 1], EPS, None, ALU.add))

        def root(k0, k1, ready):
            wait(scalar, ready)
            return act.after(scalar.activation(s["rstd"][:, k0:k1], s["rstd"][:, k0:k1], ACT.Sqrt))

        def normalise(y, k0, k1, ready):
            at = slice(k0, k1)
            wait(vector, ready)
            m = chain([
                lambda: vector.reciprocal(s["rstd"][:, at], s["rstd"][:, at]),
                lambda: vector.scalar_tensor_tensor(out=s["centre"][:, at], in0=moments[:, at, 0], scalar=-1.0,
                                                    in1=s["rstd"][:, at], op0=ALU.mult, op1=ALU.mult),
            ])
            wait(scalar, m)
            for k in range(k0, k1):
                m = act.after(scalar.activation(y[:, k, :], y[:, k, :], ACT.Identity, bias=s["centre"][:, k:k + 1],
                                                scale=s["rstd"][:, k:k + 1]))
            return m

        evac_free, was_split = {}, {}
        rest_space = pair[:, :, :].rearrange("p s l -> p (s l)").bitcast(F32)

        def project(layer, source, function, k0, k1, ready):
            w, turned = conv_w[layer], ring_b[:, 0:NP]
            wait(tensor, ready)
            for q, c0 in enumerate(range(k0, k1, 4)):
                bank, n = 6 + q % 2, min(4, k1 - c0)
                if bank in evac_free:
                    wait(tensor, evac_free[bank])
                for k in range(c0, c0 + n):
                    mark = pe.after(tensor.transpose(ps[bank][:, (k - c0) * P:(k - c0 + 1) * P], source[:, k, 0:F], ident[:, :]))
                wait(scalar, mark)
                evac_free[bank] = act.after(scalar.activation(turned[:, c0 * P:(c0 + n) * P], ps[bank][:, 0:n * P], function))
            wait(tensor, evac_free[bank], w_made[layer])
            for q, c0 in enumerate(range(k0, k1, 3)):
                bank, n = 2 + q % 2, min(3, k1 - c0)
                if bank in evac_free:
                    wait(tensor, evac_free[bank])
                for i in range(n):
                    mark = pe.after(tensor.matmul(ps[bank][:, i * W:(i + 1) * W], lhsT=turned[:, (c0 + i) * P:(c0 + i + 1) * P],
                                                  rhs=w[:, :], start=True, stop=True))
                wait(vector, mark)
                blk = ps[bank][:, 0:n * W].rearrange("p (k f) -> p k f", f=W)
                vec.after(vector.tensor_copy(tab[:, c0:c0 + n, F + 1], blk[:, :, F]))
                mark = vec.after(vector.tensor_copy(s["ad"][:, c0:c0 + n], blk[:, :, F + 1]))
                wait(scalar, mark)
                evac_free[bank] = act.after(scalar.activation(tab[:, c0:c0 + n, 0:F], blk[:, :, 0:F], ACT.Copy))
            at, rest = slice(k0, k1), rest_space[:, 0:(k1 - k0) * W].rearrange("p (k f) -> p k f", f=W)
            wait(scalar, evac_free[bank])
            m = act.after(scalar.activation(split[:, at, 0, :], tab[:, at, :], ACT.Copy))
            wait(vector, m)
            m = vec.after(vector.tensor_tensor(rest, tab[:, at, :], split[:, at, 0, :], ALU.subtract))
            wait(scalar, m)
            m = act.after(scalar.activation(split[:, at, 1, :], rest, ACT.Copy))
            wait(vector, m)
            was_split[0] = vec.after(vector.tensor_tensor(split[:, at, 2, :], rest, split[:, at, 1, :], ALU.subtract))
            wait(scalar, was_split[0])
            wait(sync, evac_free[bank])
            h_stored = stores["h"].after(sync.dma_start(
                H_table.rearrange("(k p) f -> p k f", p=P)[:, k0:k1, :], tab[:, k0:k1, :]), 16)
            wait(pool, mark, zero_stored)
            for k in range(k0, k1):
                scattered = stores["adscatter"].after(pool.indirect_dma_start(
                    out=ad_edges, out_offset=bass.IndirectOffsetOnAxis(ap=start_i[:, k:k + 1], axis=0),
                    in_=s["ad"][:, k:k + 1], in_offset=None, bounds_check=P * L - 1, oob_is_err=False), 16)
            return h_stored, scattered

        E = nodes(ring_a, F)
        wait(pool, *list(stored.values())[-RING:], placed[last_quad])
        for b in range(len(batches)):
            gather_ends(run_max, E, b)
        wait(vector, scan_done[last_quad])
        ones_col = vec.after(vector.memset(tab[:, :, F:F + 1], 1.0))
        wait(sync, ones_col)
        wait(scalar, scan_done[last_quad])
        for b, (k0, k1) in enumerate(batches):
            wait(vector, ends_got[b])
            for k in range(k0, k1):
                m = vec.after(vector.scalar_tensor_tensor(out=E[:, k, :], in0=E[:, k, :], scalar=s["negE"][:, k:k + 1],
                                                          in1=bias["b3"][:, :], op0=ALU.add, op1=ALU.add))
            wait(vector, m)
            m = vec.after(vector.scalar_tensor_tensor(out=x_sb[:, k0:k1, :], in0=E[:, k0:k1, :], scalar=0.0,
                                                      in1=x_sb[:, k0:k1, :], op0=ALU.max, op1=ALU.add))
            wait(vector, m)
            m = spread_of(x_sb, k0, k1)
            if b >= 1:
                project(0, x_sb, ACT.Copy, *batches[b - 1], normal)
            normal = normalise(x_sb, k0, k1, root(k0, k1, m))
        h_stored, scattered = project(0, x_sb, ACT.Copy, *batches[-1], normal)
        e_read = m

        wait(sync, gathered[len(groups) - 1])
        src_ready = loads["x"].after(sync.dma_start(src_i[:, :], t["src"]), 16)
        wait(pool, src_ready)
        for layer in range(2):
            wait(sync, scattered)
            m = loads["ad"].after(sync.dma_start(ad_exp[:, :], ad_edges.rearrange("(p l) a -> p (l a)", p=P)), 16)
            wait(pool, scattered)
            m2 = loads["adx"].after(pool.indirect_dma_start(out=ad_first[:, :], out_offset=None, in_=ad_edges,
                                    in_offset=bass.IndirectOffsetOnAxis(ap=first_start_i[:, :], axis=0)), 16)
            wait(vector, m, m2, evac_free[2], evac_free[3], evac_free[6], evac_free[7])
            own_score = two[:, 1, :]
            chain([
                lambda: vector.tensor_tensor(own_score, tab[:, :, F + 1], s["ad"][:, :], ALU.add),
                lambda: vector.scalar_tensor_tensor(out=own_score, in0=own_score, scalar=SLOPE, in1=own_score,
                                                    op0=ALU.mult, op1=ALU.max),
                lambda: vector.tensor_tensor(s["ad_end"][:, :], s["ad"][:, :], s["negE"][:, :], ALU.add),
            ])
            keep = ring_b[:, 0:L]
            chain([
                lambda: vector.tensor_scalar(keep, neg[:, :], 0.0, None, ALU.is_ge),
                lambda: vector.tensor_copy(ad_exp[:, 0:1], ad_first[:, :]),
                lambda: vector.tensor_tensor_scan(ring_b[:, L:2 * L], keep, ad_exp[:, :], 0.0, ALU.mult, ALU.add),
                lambda: vector.tensor_copy(ad_exp[:, :], ring_b[:, L:2 * L]),
            ])

            h_ring = ring_a[:, 0:RING1 * G1 * W].rearrange("p (s g f) -> p s g f", s=RING1, f=W)
            r_ring = ring_b[:, 0:RING1 * G1 * W].rearrange("p (s g f) -> p s g f", s=RING1, f=W)
            wait(pool, h_stored, e_read, evac_free[6], evac_free[7])
            h_free, s_stored, w_used = {}, {}, {}
            row_got, picked, picked_row, row_used, coded, last_hot = {}, {}, {}, {}, {}, {}
            by_product = [g for g, (j0, j1) in enumerate(groups1) if j1 - j0 == G1 and g >= 2]
            hot_space = [x[:, RING1 * G1 * W:NB * W].bitcast(BF16)[:, 0:4 * PIECE * P].rearrange("p (c k e) -> p c k e", c=4, e=P)
                         for x in (ring_a, ring_b)]

            def code_of(g):
                wait(scalar, row_got[g])
                if g - 1 in last_hot:
                    wait(scalar, last_hot[g - 1])
                for c in range(LAST_PIECE + 1):
                    row_used[g] = act.after(scalar.activation(code[:, c, :], src_row[:, g % 2, :], ACT.Identity,
                                                              bias=code_bias[:, c:c + 1]))
                coded[g] = row_used[g]

            def load_src_row(g):
                if g - 2 in row_used:
                    wait(sync, row_used[g - 2])
                j = groups1[g][1] - 1
                row_got[g] = row_sem[g % 2].after(sync.dma_start(
                    src_row[:, g % 2, :], t["srcL"][j:j + 1, :].to_broadcast([P, P])), 16)

            def pick(g, c):
                k0, k1 = c * PIECE, min((c + 1) * PIECE, NB)
                wait(vector, coded[g])
                if (g - 1, c) in picked:
                    wait(vector, picked[g - 1, c])
                hot = hot_space[c // 4][:, c % 4, 0:k1 - k0, :]
                last_hot[g] = vec.after(vector.tensor_tensor(hot, code[:, c:c + 1, :].to_broadcast([P, k1 - k0, P]),
                                                             block_at[:, 0:k1 - k0, :], ALU.is_equal))
                if c == 0 and g - 2 in picked_row:
                    wait(tensor, picked_row[g - 2])
                wait(tensor, last_hot[g])
                for k in range(k0, k1):
                    picked[g, c] = pe.after(tensor.matmul(ps[g % 2][:, 0:3 * W], lhsT=hot[:, k - k0, :],
                                                          rhs=split[:, k, :, :].rearrange("p s f -> p (s f)"),
                                                          start=(k == 0), stop=(k == NB - 1)))

            def put_row(g):
                slot = g % RING1
                if slot in h_free:
                    wait(scalar, h_free[slot])
                wait(scalar, picked[g, LAST_PIECE])
                evacuated[g] = act.after(scalar.activation(h_ring[:, slot, G1 - 1, :], ps[g % 2][:, 0:W], ACT.Copy))

            def add_parts(g):
                row = h_ring[:, g % RING1, G1 - 1, :]
                wait(vector, evacuated[g])
                m = vec.after(vector.tensor_tensor(row, row, ps[g % 2][:, W:2 * W], ALU.add))
                wait(vector, m)
                picked_row[g] = vec.after(vector.tensor_tensor(row, row, ps[g % 2][:, 2 * W:3 * W], ALU.add))

            evacuated = {}
            wait(vector, evac_free[6], evac_free[7], evac_free[2], evac_free[3])
            wait(tensor, was_split[0], evac_free[2], evac_free[3])
            wait(scalar, e_read)
            load_src_row(2)
            code_of(2)
            load_src_row(3)
            previous, prev_max = zero_tile[:, 0:F + 1], zero_tile[:, F + 1:W]
            m = vec.after(vector.memset(gmm[:, 1, G1:G1 + 1], 0.0))
            wait(vector, m)
            pn = G1
            for g, (j0, j1) in enumerate(groups1):
                slot, n, par = g % RING1, j1 - j0, g % 2
                if slot in h_free:
                    wait(pool, h_free[slot])
                by_dma = j1 - 1 if g in by_product else j1
                for j in range(j0, by_dma):
                    got = q_sem[slot].after(pool.indirect_dma_start(
                        out=h_ring[:, slot, j - j0, :], out_offset=None, in_=H_table,
                        in_offset=bass.IndirectOffsetOnAxis(ap=src_i[:, j:j + 1], axis=0)), 16)
                wait(vector, got)
                if g in by_product:
                    wait(vector, picked_row[g])
                if slot in s_stored:
                    wait(vector, s_stored[slot])
                a_src = h_ring[:, slot, 0:n, F + 1]
                top = r_ring[:, slot, 0:n, F + 1]
                ngs, ads = neg[:, j0:j1], ad_exp[:, j0:j1]
                mm = gmm[:, par, :]
                m = vec.after(vector.tensor_tensor_scan(top, ngs, a_src, prev_max, ALU.add, ALU.max))
                m2 = vec.after(vector.tensor_tensor(gz[:, 0:n], a_src, ads, ALU.add))
                wait(vector, m)
                m3 = vec.after(vector.tensor_tensor(gd[:, 0:n], top, ads, ALU.add))
                vec.after(vector.tensor_copy(mm[:, 0:1], gmm[:, 1 - par, pn:pn + 1]))
                wait(vector, m3)
                vec.after(vector.scalar_tensor_tensor(out=mm[:, 1:n + 1], in0=gd[:, 0:n], scalar=SLOPE, in1=gd[:, 0:n],
                                                      op0=ALU.mult, op1=ALU.max))
                m2 = vec.after(vector.scalar_tensor_tensor(out=gw[:, 0:n], in0=gz[:, 0:n], scalar=SLOPE, in1=gz[:, 0:n],
                                                           op0=ALU.mult, op1=ALU.max))
                wait(vector, m2)
                if par in w_used:
                    wait(vector, w_used[par])
                vec.after(vector.tensor_tensor(ge[:, par, 0:n], gw[:, 0:n], mm[:, 1:n + 1], ALU.subtract))
                m = vec.after(vector.tensor_tensor(gz[:, 0:n], mm[:, 0:n], mm[:, 1:n + 1], ALU.subtract))
                wait(vector, m)
                m = vec.after(vector.tensor_tensor(gc[:, par, 0:n], gz[:, 0:n], ngs, ALU.add))
                wait(scalar, m)
                act.after(scalar.activation(ge[:, par, 0:n], ge[:, par, 0:n], ACT.Exp))
                m = act.after(scalar.activation(gc[:, par, 0:n], gc[:, par, 0:n], ACT.Exp))
                wait(scalar, m)
                if g + 2 in by_product:
                    pick(g + 2, 0)
                wait(vector, m)
                for i in range(n):
                    scaled = act.after(scalar.activation(h_ring[:, slot, i, 0:F + 1], h_ring[:, slot, i, 0:F + 1], ACT.Copy,
                                                         scale=ge[:, par, i:i + 1]))
                    wait(vector, scaled)
                    last = vec.after(vector.scalar_tensor_tensor(
                        out=r_ring[:, slot, i, 0:F + 1], in0=previous, scalar=gc[:, par, i:i + 1],
                        in1=h_ring[:, slot, i, 0:F + 1], op0=ALU.mult, op1=ALU.add))
                    previous = r_ring[:, slot, i, 0:F + 1]
                    if g + 2 in by_product and i + 1 <= LAST_PIECE:
                        pick(g + 2, i + 1)
                    wait(vector, last)
                    if g + 1 in by_product and i == 7:
                        put_row(g + 1)
                    if g + 1 in by_product and i == 9:
                        add_parts(g + 1)
                    if g + 3 in by_product and i == 9:
                        code_of(g + 3)
                prev_max = r_ring[:, slot, n - 1, F + 1:W]
                whole_last = r_ring[:, slot, n - 1, :]
                pn = n
                w_used[par] = scaled
                h_free[slot] = last
                if g + 4 in by_product:
                    load_src_row(g + 4)
                wait(sync, last)
                s_stored[slot] = s_sem[slot].after(sync.dma_start(
                    run_sum.rearrange("(p l) f -> p l f", p=P)[:, j0:j1, :], r_ring[:, slot, 0:n, :]), 16)

            skipped = vec.after(vector.memset(fix[:, :], 0.0))
            wait(pool, skipped, *s_stored.values())
            fix_got = loads["fix"].after(pool.indirect_dma_start(
                out=fix[:, :], out_offset=None, in_=run_sum, in_offset=bass.IndirectOffsetOnAxis(ap=fix_i[:, :], axis=0),
                bounds_check=P * L - 1, oob_is_err=False), 16)

            wait(tensor, last)
            pe.after(tensor.transpose(ps[4][:, 0:P], whole_last[:, 0:F], ident[:, :]))
            spread(whole_last[:, F + 1:W], ps[5][:, 0:P])
            spread(ad_exp[:, L - 1:L], ps[6][:, 0:P])
            m = spread(whole_last[:, F:F + 1], ps[7][:, 0:P])
            wait(vector, m)
            m = chain([
                lambda: vector.tensor_copy(r["adl"][:, :], ps[6][:, 0:P]),
                lambda: vector.tensor_tensor_scan(r["rs"][:, :], r["link"][:, :], ps[5][:, 0:P], -BIG, ALU.add, ALU.max),
                lambda: vector.tensor_tensor(r["ma"][:, :], ps[5][:, 0:P], r["adl"][:, :], ALU.add),
                lambda: vector.scalar_tensor_tensor(out=r["ma"][:, :], in0=r["ma"][:, :], scalar=SLOPE, in1=r["ma"][:, :], op0=ALU.mult, op1=ALU.max),
                lambda: vector.tensor_tensor(r["ms"][:, :], r["rs"][:, :], r["adl"][:, :], ALU.add),
                lambda: vector.scalar_tensor_tensor(out=r["ms"][:, :], in0=r["ms"][:, :], scalar=SLOPE, in1=r["ms"][:, :], op0=ALU.mult, op1=ALU.max),
                lambda: vector.tensor_tensor(r["ma"][:, :], r["ma"][:, :], r["ms"][:, :], ALU.subtract),
                lambda: vector.memset(r["cc"][:, :], 0.0),
                lambda: vector.tensor_tensor(r["cc"][:, 1:P], r["ms"][:, 0:P - 1], r["ms"][:, 1:P], ALU.subtract),
                lambda: vector.tensor_tensor(r["cc"][:, :], r["cc"][:, :], r["link"][:, :], ALU.add),
            ])
            wait(scalar, m)
            act.after(scalar.activation(r["ma"][:, :], r["ma"][:, :], ACT.Exp))
            m = act.after(scalar.activation(r["cc"][:, :], r["cc"][:, :], ACT.Exp))
            wait(vector, m)
            m = chain([
                lambda: vector.tensor_tensor(r["l"][:, :], ps[7][:, 0:P], r["ma"][:, :], ALU.mult),
                lambda: vector.tensor_tensor(r["ma"][:, :], ps[4][:, 0:P], r["ma"][:, :], ALU.mult),
                lambda: vector.memset(state_shift[:, :, :], 0.0),
                lambda: vector.tensor_tensor_scan(state[:, :], r["cc"][:, :], r["ma"][:, :], 0.0, ALU.mult, ALU.add),
                lambda: vector.tensor_copy(state_shift[:, 0, 1:P], state[:, 0:P - 1]),
                lambda: vector.tensor_tensor_scan(state[:, :], r["cc"][:, :], r["l"][:, :], 0.0, ALU.mult, ALU.add),
                lambda: vector.tensor_copy(state_shift[:, 1, 1:P], state[:, 0:P - 1]),
                lambda: vector.tensor_copy(state_shift[:, 2, 1:P], r["rs"][:, 0:P - 1]),
            ])
            wait(tensor, m)
            for i in range(3):
                m = pe.after(tensor.transpose(ps[4 + i][:, 0:P], state_shift[:, i, :], ident[:, :]))
            wait(vector, m, fix_got)
            ad_f = ad_first[:, 0:1]
            sc = fix_s
            m = chain([
                lambda: vector.tensor_copy(sc[:, 0:1], fix[:, F + 1:W]),
                lambda: vector.tensor_copy(sc[:, 1:2], ps[6][:, 0:1]),
                lambda: vector.tensor_tensor(sc[:, 2:3], sc[:, 0:1], sc[:, 1:2], ALU.max),
                lambda: vector.tensor_copy(fix[:, F + 1:W], sc[:, 2:3]),
                lambda: vector.tensor_scalar(sc[:, 0:3], sc[:, 0:3], ad_f, None, ALU.add),
                lambda: vector.scalar_tensor_tensor(out=sc[:, 0:3], in0=sc[:, 0:3], scalar=SLOPE, in1=sc[:, 0:3], op0=ALU.mult, op1=ALU.max),
                lambda: vector.tensor_scalar(sc[:, 3:5], sc[:, 0:2], sc[:, 2:3], None, ALU.subtract),
            ])
            wait(scalar, m)
            m = act.after(scalar.activation(sc[:, 3:5], sc[:, 3:5], ACT.Exp))
            wait(vector, m)
            m = chain([
                lambda: vector.tensor_scalar(fix[:, 0:F + 1], fix[:, 0:F + 1], sc[:, 3:4], None, ALU.mult),
                lambda: vector.scalar_tensor_tensor(out=fix[:, 0:F], in0=ps[4][:, 0:F], scalar=sc[:, 4:5], in1=fix[:, 0:F],
                                                    op0=ALU.mult, op1=ALU.add),
                lambda: vector.scalar_tensor_tensor(out=fix[:, F:F + 1], in0=ps[5][:, 0:1], scalar=sc[:, 4:5], in1=fix[:, F:F + 1],
                                                    op0=ALU.mult, op1=ALU.add),
            ])
            wait(pool, m)
            fixed = stores["fix"].after(pool.indirect_dma_start(
                out=run_sum, out_offset=bass.IndirectOffsetOnAxis(ap=fix_i[:, :], axis=0), in_=fix[:, :], in_offset=None,
                bounds_check=P * L - 1, oob_is_err=False), 16)

            E = nodes(ring_a, W)
            wait(pool, fixed)
            for b in range(len(batches)):
                gather_ends(run_sum, E, b)
            name = "c1" if layer == 0 else "c2"
            spreads, roots = {}, {}

            def write_out(b):
                k0, k1 = batches[b]
                k2 = min(k1, FULL)
                wait(sync, normalise(x_sb, k0, k1, roots[b]))
                written = stores["out"].after(sync.dma_start(
                    out[k0 * P:k2 * P, :].rearrange("(k p) f -> p k f", p=P), x_sb[:, k0:k2, :]), 16)
                if k1 > FULL:
                    written = stores["out"].after(sync.dma_start(out[FULL * P:N, :], x_sb[0:REST, FULL, :]), 16)
                return written

            wait(scalar, h_stored)
            for b, (k0, k1) in enumerate(batches):
                wait(vector, ends_got[b])
                at, n = slice(k0, k1), k1 - k0
                end_score, own_score, top, both = two[:, 0, at], two[:, 1, at], s["s0"][:, at], two[:, :, at]
                m = chain([
                    lambda: vector.tensor_tensor(end_score, E[:, at, F + 1], s["ad_end"][:, at], ALU.add),
                    lambda: vector.scalar_tensor_tensor(out=end_score, in0=end_score, scalar=SLOPE, in1=end_score,
                                                        op0=ALU.mult, op1=ALU.max),
                    lambda: vector.tensor_tensor(top, end_score, own_score, ALU.max),
                    lambda: vector.tensor_tensor(both, both, top.unsqueeze(1).to_broadcast([P, 2, n]), ALU.subtract),
                ])
                wait(scalar, m)
                m = act.after(scalar.activation(both, both, ACT.Exp))
                wait(vector, m)
                m = chain([
                    lambda: vector.tensor_tensor(s["s3"][:, at], E[:, at, F], end_score, ALU.mult),
                    lambda: vector.tensor_tensor(s["s3"][:, at], s["s3"][:, at], own_score, ALU.add),
                    lambda: vector.reciprocal(s["s3"][:, at], s["s3"][:, at]),
                    lambda: vector.tensor_tensor(both, both, s["s3"][:, at].unsqueeze(1).to_broadcast([P, 2, n]), ALU.mult),
                ])
                wait(scalar, m)
                for k in range(k0, k1):
                    own = act.after(scalar.activation(tab[:, k, 0:F], tab[:, k, 0:F], ACT.Copy, scale=two[:, 1, k:k + 1]))
                    wait(vector, own)
                    m = vec.after(vector.scalar_tensor_tensor(out=E[:, k, 0:F], in0=E[:, k, 0:F], scalar=two[:, 0, k:k + 1],
                                                              in1=tab[:, k, 0:F], op0=ALU.mult, op1=ALU.add))
                if layer == 1 and b >= 2:
                    write_out(b - 2)
                if layer == 1 and b >= 1:
                    roots[b - 1] = root(*batches[b - 1], spreads[b - 1])
                wait(vector, m)
                m = vec.after(vector.tensor_tensor(E[:, at, 0:F], E[:, at, 0:F],
                                                   bias[name][:, :].unsqueeze(1).to_broadcast([P, n, F]), ALU.add))
                if layer == 0:
                    if b >= 1:
                        project(1, E, ACT.Relu, *batches[b - 1], summed)
                    summed = m
                    continue
                wait(vector, m)
                m = vec.after(vector.scalar_tensor_tensor(out=x_sb[:, at, :], in0=E[:, at, 0:F], scalar=0.0,
                                                          in1=x_sb[:, at, :], op0=ALU.max, op1=ALU.add))
                wait(vector, m)
                spreads[b] = spread_of(x_sb, k0, k1)
            if layer == 1:
                write_out(len(batches) - 2)
                roots[len(batches) - 1] = root(*batches[-1], spreads[len(batches) - 1])
                written = write_out(len(batches) - 1)
            if layer == 0:
                h_stored, scattered = project(1, E, ACT.Relu, *batches[-1], summed)
                e_read = m
        wait(sync, written)


_NAMES = {"x": "x", "srcT": "src", "src": "src", "srcL": "src", "dst": "dst", "W1": "L0_gnn_W1", "b1": "L0_gnn_b1", "W2": "L0_gnn_W2",
          "b2": "L0_gnn_b2", "W3": "L0_gnn_W3", "b3": "L0_gnn_b3", "C1": "L1_gnn_W1", "as1": "L1_gnn_att_src1",
          "ad1": "L1_gnn_att_dst1", "cb1": "L1_gnn_b1", "C2": "L1_gnn_W2", "as2": "L1_gnn_att_src2",
          "ad2": "L1_gnn_att_dst2", "cb2": "L1_gnn_b2"}


def kernel(**inputs):
    import numpy as np
    import concourse.bacc as bacc
    from concourse.bass_utils import run_bass_kernel_spmd

    N, F = inputs["x"].shape
    E = inputs["src"].shape[0]
    L = -(-E // 128)
    nc = bacc.Bacc("TRN2", target_bir_lowering=False, num_devices=1)
    arrays, aps = {}, {}
    for short, name in _NAMES.items():
        a = np.ascontiguousarray(inputs[name])
        if short in ("src", "srcT", "srcL", "dst"):
            a = np.concatenate([a, np.full(128 * L - E, N if short == "dst" else 0, a.dtype)]).reshape(128, L)
            if short == "srcT":
                a = np.ascontiguousarray(a.reshape(L, 128).T)
            if short == "srcL":
                a = np.ascontiguousarray(a.T)
        arrays[f"in_{short}"] = a
        aps[short] = nc.dram_tensor(f"in_{short}", a.shape, mybir.dt.from_np(a.dtype), kind="ExternalInput").ap()
    out = nc.dram_tensor("out", (N, F), F32, kind="ExternalOutput").ap()
    edge_network(nc, aps, out)
    result = run_bass_kernel_spmd(nc, [arrays], core_ids=[0])
    return result.results[0]["out"]
```
